# Optimizing a Trainium2 kernel written in Bass

```python
import numpy as np
import jax
import jax.numpy as jnp

def _softmax(x, axis=-1):
    return jax.nn.softmax(x, axis=axis)

def _gelu(x):
    return jax.nn.gelu(x, approximate=True)

def _silu(x):
    return jax.nn.silu(x)

def _sigmoid(x):
    return jax.nn.sigmoid(x)

def _layernorm(x, axis=-1, eps=1e-05):
    m = jnp.mean(x, axis=axis, keepdims=True)
    v = jnp.var(x, axis=axis, keepdims=True)
    return (x - m) / jnp.sqrt(v + eps)

def _scatter_add(tgt, idx, src, axis=0):
    return tgt.at[idx].add(src)

def _segment_sum(src, seg, n):
    return jax.ops.segment_sum(src, seg, n)
kernel_name = 'mk_gnn_preln_d1_gnn_r32_0dda8d'

def setup_inputs(seed: int=0):
    np.random.seed(seed)
    _w = jnp.asarray

    def _rec_inputs():
        import jax
        import jax.numpy as jnp
        _gk = jax.random.key(seed)
        x = -0.0001006 + 1 * jax.random.normal(jax.random.fold_in(_gk, 1), (3125, 96), jnp.float32)
        _s = jax.random.randint(jax.random.fold_in(_gk, 2), (50000,), 0, 3125, jnp.int32)
        _d = jax.random.randint(jax.random.fold_in(_gk, 3), (50000,), 0, 3125, jnp.int32)
        _loop = jnp.arange(3125, dtype=jnp.int32)
        src = jnp.concatenate([_s, _d, _loop])
        dst = jnp.concatenate([_d, _s, _loop])
        _o = jnp.argsort(dst, stable=True)
        src = src[_o]
        dst = dst[_o]
        edge_attr_17 = jax.random.uniform(jax.random.fold_in(_gk, 11), (103125, 17), jnp.float32, 0.0, 1)
        return (x, src, dst, edge_attr_17)
    x, src, dst, edge_attr_17 = _rec_inputs()

    def _L0_gnn_setup():
        import jax, jax.numpy as jnp
        import numpy as np
        N = 50000
        E = 25000
        D = 96
        ED = 17
        key = jax.random.key(seed)
        ks = jax.random.split(key, 12)
        x = jax.random.normal(ks[0], (N, D), dtype=jnp.float32)
        edge_index = jax.random.randint(ks[1], (2, E), 0, N, dtype=jnp.int64)
        edge_attr = jax.random.uniform(ks[2], (E, ED), dtype=jnp.float32)
        s = 1.0 / np.sqrt(ED)
        W1 = jax.random.uniform(ks[3], (D, ED), jnp.float32, -s, s)
        b1 = jax.random.uniform(ks[4], (D,), jnp.float32, -s, s)
        s = 1.0 / np.sqrt(D)
        W2 = jax.random.uniform(ks[5], (D, D), jnp.float32, -s, s)
        b2 = jax.random.uniform(ks[6], (D,), jnp.float32, -s, s)
        Ws = jax.random.uniform(ks[7], (D, D), jnp.float32, -s, s)
        bs = jax.random.uniform(ks[8], (D,), jnp.float32, -s, s)
        Wn = jax.random.uniform(ks[9], (D, D), jnp.float32, -s, s)
        bn = jax.random.uniform(ks[10], (D,), jnp.float32, -s, s)
        return {'x': x, 'edge_index': edge_index, 'edge_attr': edge_attr, 'W1': W1, 'b1': b1, 'W2': W2, 'b2': b2, 'Ws': Ws, 'bs': bs, 'Wn': Wn, 'bn': bn}
    _L0_gnn_all = _L0_gnn_setup()
    _L0_gnn_in = {k: v for k, v in _L0_gnn_all.items() if k in ('W1', 'b1', 'W2', 'b2', 'Ws', 'bs', 'Wn', 'bn')}
    del _L0_gnn_all
    return {'x': x, 'src': src, 'dst': dst, 'edge_attr_17': edge_attr_17, 'L0_gnn_W1': _L0_gnn_in['W1'], 'L0_gnn_b1': _L0_gnn_in['b1'], 'L0_gnn_W2': _L0_gnn_in['W2'], 'L0_gnn_b2': _L0_gnn_in['b2'], 'L0_gnn_Ws': _L0_gnn_in['Ws'], 'L0_gnn_bs': _L0_gnn_in['bs'], 'L0_gnn_Wn': _L0_gnn_in['Wn'], 'L0_gnn_bn': _L0_gnn_in['bn']}

def reference(x, src, dst, edge_attr_17, L0_gnn_W1, L0_gnn_b1, L0_gnn_W2, L0_gnn_b2, L0_gnn_Ws, L0_gnn_bs, L0_gnn_Wn, L0_gnn_bn):
    import jax
    import jax.numpy as jnp

    def _L0_gnn_ref(x, edge_index, edge_attr, W1, b1, W2, b2, Ws, bs, Wn, bn):
        import jax, jax.numpy as jnp
        import numpy as np
        N = 50000
        E = 25000
        D = 96
        ED = 17
        src, dst = (edge_index[0], edge_index[1])
        h = jax.nn.relu(edge_attr @ W1.T + b1)
        w = h @ W2.T + b2
        msg = w * x[src]
        agg = jax.ops.segment_sum(msg, dst, num_segments=x.shape[0])
        return jax.nn.relu(x @ Ws.T + bs + agg @ Wn.T + bn)
    edge_index = jnp.stack([src, dst])
    h = jnp.maximum(_layernorm(x, axis=-1), 0.0)
    x = x + _L0_gnn_ref(h, edge_index, edge_attr_17, L0_gnn_W1, L0_gnn_b1, L0_gnn_W2, L0_gnn_b2, L0_gnn_Ws, L0_gnn_bs, L0_gnn_Wn, L0_gnn_bn)
    return x

_drawn_inputs = setup_inputs


def setup_inputs(seed=0):
    import zlib

    import numpy as np

    out = dict(_drawn_inputs(seed))
    spreads = {}
    factors = {}
    for name, (base, spread) in spreads.items():
        noise = np.random.default_rng([zlib.crc32(name.encode()), seed]).standard_normal(out[name].shape)
        drawn = base * np.exp(spread * noise) if base else spread * noise
        out[name] = jnp.asarray(drawn.astype(out[name].dtype))
    for name, factor in factors.items():
        out[name] = (out[name] * factor).astype(out[name].dtype)
    return out
```

```python
import concourse.bass as bass
from concourse import mybir
from contextlib import ExitStack

N, D, ED, E = 3125, 96, 17, 103125
P = 128
TILE = P
BLOCK = 4
GROUP = 8
TILES = -(-E // TILE)
PAIRS = -(-TILES // (2 * GROUP))
GROUPS = 2 * PAIRS
BLOCKS = 2 * GROUPS
TPAD = GROUPS * GROUP
EPAD = TPAD * TILE
PADS = EPAD - E
WIN = 64
SWEEP = 512
SWEEPS = -(-N // SWEEP)
AGGW = SWEEPS * SWEEP
NP = 125
NC = N // NP
assert AGGW >= N + WIN


def gnn_layer(nc, x, src_tiles, src, dst, attr, w1, b1, w2, ws, wn, out):
    fp32 = mybir.dt.float32
    i32 = mybir.dt.int32
    ALU = mybir.AluOpType
    ACT = mybir.ActivationFunctionType
    AX = mybir.AxisListType

    x_v = x.rearrange("(p c) f -> p c f", p=NP)
    out_v = out.rearrange("(p c) f -> p c f", p=NP)
    h_dram = nc.dram_tensor("h_rows", [N, D], fp32, kind="Internal").ap()
    h_v = h_dram.rearrange("(p c) f -> p c f", p=NP)

    with ExitStack() as ctx:
        def sb(name, shape, dt=fp32):
            return ctx.enter_context(nc.sbuf_tensor(name, shape, dt))

        def sem(name):
            return ctx.enter_context(nc.semaphore(name))

        w1_sb = sb("w1_sb", [ED, D])
        b1_sb = sb("b1_sb", [D, 1])
        w2_sb = sb("w2_sb", [D + 1, D])
        ws_sb = sb("ws_sb", [D + 2, D])
        wn_sb = sb("wn_sb", [D, D])
        x_sb = sb("x_sb", [NP, NC, D])
        xc_sb = sb("xc_sb", [NP, NC, D])
        sq_sb = sb("sq_sb", [NP, NC, D])
        stat = sb("stat", [NP, 4, NC])
        hT = sb("hT", [D + 2, NC, NP])
        self_sb = sb("self_sb", [NP, NC, D])
        aggT = sb("aggT", [D, AGGW])
        o_sb = sb("o_sb", [NP, NC, D])
        dst_sb = sb("dst_sb", [P, TPAD], i32)
        dstf = sb("dstf", [P, TPAD])
        local = sb("local", [P, TPAD])
        off = sb("off", [P, TPAD])
        base_b = sb("base_b", [P, GROUPS])
        base_i = sb("base_i", [1, GROUPS], i32)
        outside = sb("outside", [P, 2])
        misfits = sb("misfits", [1, 1], i32)
        iota_i = sb("iota_i", [P, SWEEP], i32)
        iota_f = sb("iota_f", [P, SWEEP])
        diff = sb("diff", [P, P], i32)
        ident = sb("ident", [P, P])
        ones = sb("ones", [P, P])
        eps = sb("eps", [P, 1])
        idx_sb = [sb(f"idx{k}", [P, GROUP], i32) for k in range(2)]
        attr_sb = [sb(f"attr{k}", [ED, GROUP * TILE]) for k in range(2)]
        g_sb = [sb(f"gathered{k}", [P, GROUP, D]) for k in range(2)]
        r_sb = [sb(f"relu{k}", [D + 1, BLOCK * TILE]) for k in range(2)]
        msg = [sb(f"msg{k}", [P, BLOCK, D]) for k in range(2)]
        hot = [sb(f"hot{k}", [P, GROUP, WIN]) for k in range(2)]
        idx1 = sb("idx_one", [P, 1], i32)
        dst1 = sb("dst1", [P, 1])
        hot1 = sb("hot_sweep", [P, SWEEP])

        ps_l1 = [ctx.enter_context(nc.psum_tensor(f"ps_l1{k}", [P, 512], fp32)) for k in range(2)]
        ps_l2 = [ctx.enter_context(nc.psum_tensor(f"ps_l2{k}", [P, 512], fp32)) for k in range(2)]
        ps_ag = [ctx.enter_context(nc.psum_tensor(f"ps_ag{k}", [P, 512], fp32)) for k in range(2)]
        ps_o = [ctx.enter_context(nc.psum_tensor(f"ps_o{k}", [P, 512], fp32)) for k in range(2)]

        x_in, weights_in, dst_in, h_out, stored = (
            sem(n) for n in ("x_in", "weights_in", "dst_in", "h_out", "stored"))
        v_step = sem("v_step")
        rows_of_ones = sem("rows_of_ones")
        consts, diffs, std_done, h_ready = (sem(n) for n in ("consts", "diffs", "std_done", "h_ready"))
        var_done, dstf_ready, base_ps, base_ready, outside_ready, count_ps, flag_ready = (
            sem(n) for n in ("var_done", "dstf_ready", "base_ps", "base_ready", "outside_ready",
                             "count_ps", "flag_ready"))
        ht_ps, ht_sb, self_ps, self_done, local_ready = (
            sem(n) for n in ("ht_ps", "ht_sb", "self_ps", "self_done", "local_ready"))
        idx_in = [sem(f"idx_in{k}") for k in range(2)]
        attr_in = [sem(f"attr_in{k}") for k in range(2)]
        gathered = [sem(f"gathered{k}_in") for k in range(2)]
        l1_done, relu_done, l2_done, msg_done, hot_done, scat_done, agg_done = (
            sem(n) for n in ("l1_done", "relu_done", "l2_done", "msg_done", "hot_done", "scat_done",
                             "agg_done"))
        out_ps, out_ready = sem("out_ps"), sem("out_ready")
        m_attr, m_idx, m_gather, m_l1, m_relu, m_l2, m_msg, m_hot, m_scat, m_agg, m_dst, m_mask = (
            sem("m_" + n) for n in ("attr", "idx", "gather", "l1", "relu", "l2", "msg", "hot", "scat",
                                    "agg", "dst", "mask"))
        block = ctx.enter_context(nc.Block())

        def flag_on(eng):
            eng.wait_ge(flag_ready, 1)
            return eng.value_load(misfits[0:1, 0:1], min_val=0, max_val=EPAD)

        @block.sync
        def _(sp):
            sp.dma_start(x_sb[0:112], x_v[0:112]).then_inc(x_in, 16)
            sp.dma_start(x_sb[112:NP], x_v[112:NP]).then_inc(x_in, 16)

            def load_idx(i, k):
                if not (isinstance(i, int) and i == 0):
                    sp.wait_ge(gathered[k], 16 * GROUP * i)
                sp.dma_start(idx_sb[k][:, :], src[2 * i + k]).then_inc(idx_in[k], 16)

            def load_attr(i, k):
                if not (isinstance(i, int) and i == 0):
                    sp.wait_ge(l1_done, 4 * i + 2 * k - 2)
                cols = bass.ds((2 * i + k) * GROUP * TILE, GROUP * TILE)
                sp.dma_start(attr_sb[k][0:16, :], attr[0:16, cols]).then_inc(attr_in[k], 16)
                sp.dma_start(attr_sb[k][16:17, :].rearrange("p (a b) -> p a b", a=16),
                             attr[16:17, cols].rearrange("p (a b) -> p a b", a=16)).then_inc(attr_in[k], 16)

            load_idx(0, 0)
            load_idx(0, 1)
            load_attr(0, 0)
            load_attr(0, 1)
            sp.wait_ge(h_ready, 1)
            sp.dma_start(h_v[0:112], xc_sb[0:112]).then_inc(h_out, 16)
            sp.dma_start(h_v[112:NP], xc_sb[112:NP]).then_inc(h_out, 16)
            with sp.Fori(1, PAIRS) as i:
                for k in range(2):
                    load_idx(i, k)
                    load_attr(i, k)
            with sp.If(flag_on(sp) > 0):
                sp.wait_ge(l1_done, BLOCKS)
                with sp.Fori(0, TILES) as t:
                    sp.wait_ge(m_gather, 16 * t)
                    sp.dma_start(idx1[:, :], src_tiles[bass.ds(t, 1), :].rearrange("t p -> p t")).then_inc(m_idx, 16)
                    sp.wait_ge(m_l1, t)
                    sp.dma_start(attr_sb[0][:, 0:TILE], attr[:, bass.ds(t * TILE, TILE)]).then_inc(m_attr, 16)
            for q in range(NC // 5):
                sp.wait_ge(out_ready, q + 1)
                sp.dma_start(out_v[:, 5 * q:5 * q + 5], o_sb[:, 5 * q:5 * q + 5]).then_inc(stored, 16)
            sp.wait_ge(stored, 16 * (NC // 5))

        @block.gpsimd
        def _(pool):
            pool.memset(ones[:, :], 1.0).then_inc(consts, 1)
            pool.iota(iota_i[:, :], [[1, SWEEP]], base=0, channel_multiplier=0).then_inc(consts, 1)
            pool.iota(diff[:, :], [[1, P]], base=0, channel_multiplier=-1).then_inc(diffs, 1)
            pool.memset(aggT[:, :], 0.0).then_inc(consts, 1)

            def gather(i, k, tiles):
                if not (isinstance(i, int) and i == 0):
                    pool.wait_ge(msg_done, 4 * i + 2 * k - 2)
                pool.wait_ge(idx_in[k], 16 * i + 16)
                pool.nop(nofuse=True)
                for j in range(tiles):
                    pool.indirect_dma_start(
                        g_sb[k][:, j, :], None, h_dram[:, :],
                        bass.IndirectOffsetOnAxis(ap=idx_sb[k][:, j:j + 1], axis=0)
                    ).then_inc(gathered[k], 16)

            pool.wait_ge(h_out, 32)
            gather(0, 0, GROUP)
            gather(0, 1, GROUP)
            with pool.Fori(1, PAIRS - 1) as i:
                gather(i, 0, GROUP)
                gather(i, 1, GROUP)
            last = TILES - (GROUPS - 2) * GROUP
            gather(PAIRS - 1, 0, min(last, GROUP))
            gather(PAIRS - 1, 1, max(last - GROUP, 0))
            with pool.If(flag_on(pool) > 0):
                pool.wait_ge(msg_done, BLOCKS)
                with pool.Fori(0, TILES) as t:
                    pool.wait_ge(m_msg, t)
                    pool.wait_ge(m_idx, 16 * t + 16)
                    pool.nop(nofuse=True)
                    pool.indirect_dma_start(
                        g_sb[0][:, 0, :], None, h_dram[:, :],
                        bass.IndirectOffsetOnAxis(ap=idx1[:, :], axis=0)).then_inc(m_gather, 16)

        @block.scalar
        def _(act):
            act.dma_start(dst_sb[:, :], dst).then_inc(dst_in, 16)
            for t, a in ((w1_sb, w1), (b1_sb, b1), (w2_sb, w2), (ws_sb, ws), (wn_sb, wn)):
                act.dma_start(t[:, :], a).then_inc(weights_in, 16)
            act.wait_ge(var_done, 1)
            nc.scalar.activation(stat[:, 2, :], stat[:, 1, :], ACT.Sqrt, bias=eps[0:NP, 0:1],
                                 scale=1.0 / D).then_inc(std_done, 1)
            for q in range(7):
                n = min(4, NC - 4 * q)
                act.wait_ge(ht_ps, q + 1)
                nc.scalar.copy(hT[0:D, 4 * q:4 * q + n, :],
                               ps_o[q % 2][0:D, 0:n * NP].rearrange("p (c n) -> p c n", c=n)).then_inc(ht_sb, 1)

            act.wait_ge(weights_in, 80)

            def relu(i, k):
                act.wait_ge(l1_done, 4 * i + k + 1)
                if not (isinstance(i, int) and 4 * i + k < 2):
                    act.wait_ge(l2_done, 4 * i + k - 1)
                nc.scalar.activation(r_sb[k % 2][0:D, :], ps_l1[k % 2][0:D, :], ACT.Relu,
                                     bias=b1_sb[:, 0:1]).then_inc(relu_done, 1)

            for k in range(4):
                relu(0, k)
            with act.Fori(1, PAIRS) as i:
                for k in range(4):
                    relu(i, k)
            with act.If(flag_on(act) > 0):
                with act.Fori(0, TILES) as t:
                    act.wait_ge(m_l1, t + 1)
                    nc.scalar.activation(r_sb[0][0:D, 0:TILE], ps_l1[0][0:D, 0:TILE], ACT.Relu,
                                         bias=b1_sb[:, 0:1]).then_inc(m_relu, 1)

        @block.tensor
        def _(pe):
            pe.wait_ge(consts, 3)
            pe.wait_ge(dstf_ready, 1)
            nc.tensor.matmul(ps_l2[0][:, 0:GROUPS], ones[0:1, :], dstf[0:1, 0:TPAD:GROUP],
                             start=True, stop=True).then_inc(base_ps, 1)
            pe.wait_ge(rows_of_ones, 3)
            pe.wait_ge(outside_ready, 1)
            for k in range(2):
                mm = nc.tensor.matmul(ps_l2[1][0:1, 0:1], outside[:, k:k + 1], ones[:, 0:1],
                                      start=(k == 0), stop=(k == 1))
            mm.then_inc(count_ps, 1)
            pe.wait_ge(h_ready, 1)
            for q in range(7):
                n = min(4, NC - 4 * q)
                if q >= 2:
                    pe.wait_ge(ht_sb, q - 1)
                for c in range(n):
                    mm = nc.tensor.transpose(ps_o[q % 2][0:D, c * NP:(c + 1) * NP], xc_sb[:, 4 * q + c, :],
                                             ident[0:NP, 0:NP])
                mm.then_inc(ht_ps, 1)
            pe.wait_ge(weights_in, 80)
            pe.wait_ge(ht_sb, 7)
            for q in range(NC // 5):
                if q >= 2:
                    pe.wait_ge(self_done, q - 1)
                for c in range(5):
                    mm = nc.tensor.matmul(ps_o[q % 2][0:NP, c * D:(c + 1) * D], hT[:, 5 * q + c, :],
                                          ws_sb[:, :], start=True, stop=True)
                mm.then_inc(self_ps, 1)
            pe.wait_ge(flag_ready, 1)

            def layer1(i, k):
                if k % 2 == 0:
                    pe.wait_ge(attr_in[k // 2], 32 * i + 32)
                if not (isinstance(i, int) and 4 * i + k < 2):
                    pe.wait_ge(relu_done, 4 * i + k - 1)
                cols = slice((k % 2) * BLOCK * TILE, (k % 2 + 1) * BLOCK * TILE)
                nc.tensor.matmul(ps_l1[k % 2][0:D, :], w1_sb[:, :], attr_sb[k // 2][:, cols],
                                 start=True, stop=True).then_inc(l1_done, 1)

            def layer2(i, k):
                pe.wait_ge(relu_done, 4 * i + k + 1)
                if not (isinstance(i, int) and 4 * i + k < 2):
                    pe.wait_ge(msg_done, 4 * i + k - 1)
                for j in range(BLOCK):
                    mm = nc.tensor.matmul(ps_l2[k % 2][:, j * D:(j + 1) * D],
                                          r_sb[k % 2][:, j * TILE:(j + 1) * TILE], w2_sb[:, :],
                                          start=True, stop=True)
                mm.then_inc(l2_done, 1)

            def scatter(i, k):
                pe.wait_ge(msg_done, 4 * i + k + 1)
                if k % 2 == 0:
                    pe.wait_ge(hot_done, 2 * i + k // 2 + 1)
                    if not (isinstance(i, int) and 2 * i + k // 2 < 2):
                        pe.wait_ge(agg_done, 2 * i + k // 2 - 1)
                for j in range(BLOCK):
                    mm = nc.tensor.matmul(ps_ag[k // 2][0:D, 0:WIN], msg[k % 2][:, j, :],
                                          hot[k // 2][:, (k % 2) * BLOCK + j, :],
                                          start=(k % 2 == 0 and j == 0), stop=(k % 2 == 1 and j == BLOCK - 1))
                mm.then_inc(scat_done, 1)

            layer1(0, 0)
            layer1(0, 1)
            layer2(0, 0)
            for k in (2, 3):
                layer1(0, k)
                layer2(0, k - 1)
                scatter(0, k - 2)
            with pe.Fori(1, PAIRS) as i:
                for k in range(4):
                    layer1(i, k)
                    layer2(i - (k < 1), (k - 1) % 4)
                    scatter(i - (k < 2), (k - 2) % 4)
            layer2(PAIRS - 1, 3)
            scatter(PAIRS - 1, 2)
            scatter(PAIRS - 1, 3)
            with pe.If(flag_on(pe) > 0):
                pe.wait_ge(agg_done, GROUPS)
                with pe.Fori(0, TILES) as t:
                    pe.wait_ge(m_attr, 16 * t + 16)
                    pe.wait_ge(m_relu, t)
                    nc.tensor.matmul(ps_l1[0][0:D, 0:TILE], w1_sb[:, :], attr_sb[0][:, 0:TILE],
                                     start=True, stop=True).then_inc(m_l1, 1)
                    pe.wait_ge(m_relu, t + 1)
                    pe.wait_ge(m_msg, t)
                    nc.tensor.matmul(ps_l2[0][:, 0:D], r_sb[0][:, 0:TILE], w2_sb[:, :],
                                     start=True, stop=True).then_inc(m_l2, 1)
                    pe.wait_ge(m_msg, t + 1)
                    for w in range(SWEEPS):
                        pe.wait_ge(m_hot, SWEEPS * t + w + 1)
                        pe.wait_ge(m_agg, SWEEPS * t + w)
                        nc.tensor.matmul(ps_ag[0][0:D, :], msg[0][:, 0, :], hot1[:, :],
                                         start=True, stop=True).then_inc(m_scat, 1)
                pe.wait_ge(m_agg, SWEEPS * TILES)
            pe.wait_ge(agg_done, GROUPS)
            pe.wait_ge(self_done, NC // 5)
            for q in range(NC // 5):
                if q >= 2:
                    pe.wait_ge(out_ready, q - 1)
                for c in range(5):
                    mm = nc.tensor.matmul(ps_o[q % 2][0:NP, c * D:(c + 1) * D],
                                          aggT[:, 5 * q + c:N:NC], wn_sb[:, :], start=True, stop=True)
                mm.then_inc(out_ps, 1)

        @block.vector
        def _(dve):
            steps = [0]

            def step(ins):
                steps[0] += 1
                ins.then_inc(v_step, 1)
                dve.wait_ge(v_step, steps[0])

            v = nc.vector

            def per_node(a):
                return a.unsqueeze(2).broadcast_to([NP, NC, D])

            step(v.memset(eps[:, :], 1e-5))
            dve.wait_ge(diffs, 1)
            v.tensor_scalar(ident[:, :], diff[:, :], 0.0, None, ALU.is_equal)
            v.memset(hT[D:D + 2, :, :], 1.0).then_inc(rows_of_ones, 1)
            for k in range(2):
                v.memset(r_sb[k][D:D + 1, :], 1.0).then_inc(rows_of_ones, 1)
            dve.wait_ge(x_in, 32)
            step(v.tensor_reduce(stat[:, 0, :], x_sb[:, :, :], AX.X, ALU.add))
            step(v.tensor_scalar(stat[:, 0, :], stat[:, 0, :], 1.0 / D, None, ALU.mult))
            step(v.tensor_tensor(xc_sb[:, :, :], x_sb[:, :, :], per_node(stat[:, 0, :]), ALU.subtract))
            step(v.tensor_tensor(sq_sb[:, :, :], xc_sb[:, :, :], xc_sb[:, :, :], ALU.mult))
            v.tensor_reduce(stat[:, 1, :], sq_sb[:, :, :], AX.X, ALU.add).then_inc(var_done, 1)
            dve.wait_ge(std_done, 1)
            step(v.reciprocal(stat[:, 3, :], stat[:, 2, :]))
            step(v.tensor_tensor(sq_sb[:, :, :], xc_sb[:, :, :], per_node(stat[:, 3, :]), ALU.mult))
            v.tensor_scalar(xc_sb[:, :, :], sq_sb[:, :, :], 0.0, None, ALU.max).then_inc(h_ready, 1)

            dve.wait_ge(dst_in, 16)
            v.tensor_copy(dstf[:, :], dst_sb[:, :]).then_inc(dstf_ready, 1)
            dve.wait_ge(consts, 3)
            step(v.tensor_copy(iota_f[:, :], iota_i[:, :]))
            dve.wait_ge(base_ps, 1)
            step(v.tensor_scalar(base_b[:, :], ps_l2[0][:, 0:GROUPS], 0.0, None, ALU.max))
            step(v.tensor_copy(base_i[:, :], base_b[0:1, :]))
            step(v.tensor_tensor(local[:, :].rearrange("p (g j) -> p g j", j=GROUP),
                                 dstf[:, :].rearrange("p (g j) -> p g j", j=GROUP),
                                 base_b[:, :].unsqueeze(2).broadcast_to([P, GROUPS, GROUP]), ALU.subtract))
            step(v.tensor_scalar(off[:, :], local[:, :], float(WIN), 0.0, ALU.is_ge, ALU.add,
                                 accum_out=outside[:, 0:1]))
            v.tensor_scalar(off[:, :], local[:, :], 0.0, 0.0, ALU.is_lt, ALU.add,
                            accum_out=outside[:, 1:2]).then_inc(outside_ready, 1)
            dve.wait_ge(count_ps, 1)
            v.tensor_scalar(misfits[:, :], ps_l2[1][0:1, 0:1], float(-PADS), None, ALU.add).then_inc(flag_ready, 1)
            for q in range(NC // 5):
                dve.wait_ge(self_ps, q + 1)
                v.tensor_copy(self_sb[:, 5 * q:5 * q + 5, :],
                              ps_o[q % 2][0:NP, 0:5 * D].rearrange("p (c f) -> p c f", c=5)).then_inc(self_done, 1)

            def messages(i, k):
                dve.wait_ge(l2_done, 4 * i + k + 1)
                if k % 2 == 0:
                    full = GROUP
                    if isinstance(i, int) and i == PAIRS - 1:
                        full = max(0, min(GROUP, TILES - (2 * i + k // 2) * GROUP))
                    dve.wait_ge(gathered[k // 2], 16 * GROUP * i + 16 * full)
                if not (isinstance(i, int) and 4 * i + k < 2):
                    dve.wait_ge(scat_done, 4 * i + k - 1)
                h0 = (k % 2) * BLOCK
                v.tensor_tensor(msg[k % 2][:, :, :],
                                ps_l2[k % 2][:, 0:BLOCK * D].rearrange("p (j f) -> p j f", j=BLOCK),
                                g_sb[k // 2][:, h0:h0 + BLOCK, :], ALU.mult).then_inc(msg_done, 1)

            def one_hot(i, k):
                if not (isinstance(i, int) and 2 * i + k < 2):
                    dve.wait_ge(scat_done, 4 * i + 2 * k - 2)
                cols = bass.ds((2 * i + k) * GROUP, GROUP)
                v.tensor_tensor(hot[k][:, :, :],
                                local[:, cols].unsqueeze(2).broadcast_to([P, GROUP, WIN]),
                                iota_f[:, 0:WIN].unsqueeze(1).broadcast_to([P, GROUP, WIN]),
                                ALU.is_equal).then_inc(hot_done, 1)

            def aggregate(i, k):
                at = dve.value_load(base_i[0:1, bass.ds(2 * i + k, 1)], min_val=0, max_val=N - 1)
                dve.wait_ge(scat_done, 4 * i + 2 * k + 2)
                if not (isinstance(i, int) and 2 * i + k == 0):
                    dve.wait_ge(agg_done, 2 * i + k)
                win = aggT[:, bass.ds(at, WIN)]
                v.tensor_tensor(win, win, ps_ag[k][0:D, 0:WIN], ALU.add).then_inc(agg_done, 1)

            one_hot(0, 0)
            messages(0, 0)
            messages(0, 1)
            one_hot(0, 1)
            messages(0, 2)
            messages(0, 3)
            aggregate(0, 0)
            with dve.Fori(1, PAIRS - 1) as i:
                one_hot(i, 0)
                messages(i, 0)
                messages(i, 1)
                aggregate(i - 1, 1)
                one_hot(i, 1)
                messages(i, 2)
                messages(i, 3)
                aggregate(i, 0)
            i = PAIRS - 1
            one_hot(i, 0)
            messages(i, 0)
            messages(i, 1)
            aggregate(i - 1, 1)
            one_hot(i, 1)
            messages(i, 2)
            messages(i, 3)
            aggregate(i, 0)
            aggregate(i, 1)
            with dve.If(flag_on(dve) > 0):
                dve.wait_ge(agg_done, GROUPS)
                v.tensor_scalar(off[:, :], local[:, :], 0.0, None, ALU.is_ge).then_inc(m_mask, 1)
                dve.wait_ge(m_mask, 1)
                v.scalar_tensor_tensor(off[:, :], local[:, :], float(WIN), off[:, :], ALU.is_lt,
                                       ALU.mult).then_inc(m_mask, 1)
                dve.wait_ge(m_mask, 2)
                v.tensor_scalar(local[:, :], dstf[:, :], 1.0, None, ALU.add).then_inc(m_mask, 1)
                dve.wait_ge(m_mask, 3)
                v.tensor_tensor(off[:, :], off[:, :], local[:, :], ALU.mult).then_inc(m_mask, 1)
                dve.wait_ge(m_mask, 4)
                v.tensor_tensor(dstf[:, :], dstf[:, :], off[:, :], ALU.subtract).then_inc(m_mask, 1)
                dve.wait_ge(m_mask, 5)
                with dve.Fori(0, TILES) as t:
                    v.tensor_copy(dst1[:, :], dstf[:, bass.ds(t, 1)]).then_inc(m_dst, 1)
                    dve.wait_ge(m_l2, t + 1)
                    dve.wait_ge(m_gather, 16 * t + 16)
                    dve.wait_ge(m_scat, SWEEPS * t)
                    v.tensor_tensor(msg[0][:, 0, :], ps_l2[0][:, 0:D], g_sb[0][:, 0, :],
                                    ALU.mult).then_inc(m_msg, 1)
                    dve.wait_ge(m_dst, t + 1)
                    for w in range(SWEEPS):
                        dve.wait_ge(m_scat, SWEEPS * t + w)
                        v.tensor_scalar(hot1[:, :], iota_f[:, :], dst1[:, 0:1], float(-w * SWEEP),
                                        ALU.subtract, ALU.is_equal).then_inc(m_hot, 1)
                        dve.wait_ge(m_scat, SWEEPS * t + w + 1)
                        dve.wait_ge(m_agg, SWEEPS * t + w)
                        win = aggT[:, w * SWEEP:(w + 1) * SWEEP]
                        v.tensor_tensor(win, win, ps_ag[0][0:D, :], ALU.add).then_inc(m_agg, 1)
            for q in range(NC // 5):
                dve.wait_ge(out_ps, q + 1)
                cs = slice(5 * q, 5 * q + 5)
                step(v.tensor_tensor(sq_sb[:, cs, :], self_sb[:, cs, :],
                                     ps_o[q % 2][0:NP, 0:5 * D].rearrange("p (c f) -> p c f", c=5), ALU.add))
                v.scalar_tensor_tensor(o_sb[:, cs, :], sq_sb[:, cs, :], 0.0, x_sb[:, cs, :],
                                       ALU.max, ALU.add).then_inc(out_ready, 1)


def kernel(x, src, dst, edge_attr_17, L0_gnn_W1, L0_gnn_b1, L0_gnn_W2, L0_gnn_b2, L0_gnn_Ws, L0_gnn_bs,
           L0_gnn_Wn, L0_gnn_bn):
    import numpy as np
    import concourse.bacc as bacc
    from concourse.bass_utils import run_bass_kernel_spmd

    def by_tile(a, fill):
        a = np.asarray(a)
        return np.ascontiguousarray(np.concatenate([a, np.full(PADS, fill, a.dtype)]).reshape(TPAD, TILE).T)

    attr = np.asarray(edge_attr_17)
    attr = np.ascontiguousarray(np.concatenate([attr, np.zeros((PADS, ED), attr.dtype)]).T)
    b1, b2, bs, bn = (np.asarray(b)[None, :] for b in (L0_gnn_b1, L0_gnn_b2, L0_gnn_bs, L0_gnn_bn))
    arrays = {
        "x_in": np.ascontiguousarray(x),
        "src_tiles": np.ascontiguousarray(by_tile(src, 0).T),
        "src_groups": np.ascontiguousarray(by_tile(src, 0).reshape(TILE, GROUPS, GROUP).transpose(1, 0, 2)),
        "dst_tiles": by_tile(dst, -1),
        "attr_t": attr,
        "w1_t": np.ascontiguousarray(np.asarray(L0_gnn_W1).T),
        "b1_col": np.ascontiguousarray(b1.T),
        "w2_t": np.concatenate([np.asarray(L0_gnn_W2).T, b2]),
        "ws_t": np.concatenate([np.asarray(L0_gnn_Ws).T, bs, bn]),
        "wn_t": np.ascontiguousarray(np.asarray(L0_gnn_Wn).T),
    }
    nc = bacc.Bacc("TRN2", target_bir_lowering=False, num_devices=1)
    args = [nc.dram_tensor(n, a.shape, mybir.dt.from_np(a.dtype), kind="ExternalInput").ap()
            for n, a in arrays.items()]
    out = nc.dram_tensor("out_rows", [N, D], mybir.dt.float32, kind="ExternalOutput").ap()
    gnn_layer(nc, *args, out)
    r = run_bass_kernel_spmd(nc, [arrays], core_ids=[0])
    return r.results[0]["out_rows"]
```

```python
import concourse.bass as bass
from concourse import mybir
from contextlib import ExitStack

N, D, ED, E = 3125, 96, 17, 103125
P = 128
TILE = P
BLOCK = 4
HALF = 4
HTILES = BLOCK * HALF
UNIT = 2 * HALF
TILES = -(-E // TILE)
BLOCKS = -(-TILES // BLOCK)
UNITS = BLOCKS // UNIT
REST = BLOCKS - UNITS * UNIT
HALVES = -(-BLOCKS // HALF)
TPAD = HALVES * HTILES
PADS = TPAD * TILE - E
BPAD = HALVES * HALF
PEG = 2
SWG = HTILES - PEG
WIN = 32
SWEEP = 512
SWEEPS = -(-N // SWEEP)
AGGW = SWEEPS * SWEEP
NP = 125
NC = N // NP
NQ = NC // 5
NPARTS = 3
A_PART = [0, 0, 0, 1, 1, 1, 2]
W_PART = [0, 1, 2, 0, 1, 2, 0]
KA = len(A_PART) * ED
KS = KA + NPARTS
assert AGGW >= N + WIN and KS <= P and 0 < REST <= HALF and TILES - UNITS * UNIT * BLOCK <= SWG


def gnn_layer(nc, x, src, src_rows, dst, attr, attr_rows, w1, w1_part, b1, w2, ws, wn, out):
    fp32, bf16, fp16, i32 = (mybir.dt.float32, mybir.dt.bfloat16, mybir.dt.float16, mybir.dt.int32)
    ALU = mybir.AluOpType
    ACT = mybir.ActivationFunctionType
    AX = mybir.AxisListType

    x_v = x.rearrange("(p c) f -> p c f", p=NP)
    out_v = out.rearrange("(p c) f -> p c f", p=NP)
    h_dram = nc.dram_tensor("h_rows", [N, D], fp32, kind="Internal").ap()
    h_v = h_dram.rearrange("(p c) f -> p c f", p=NP)

    with ExitStack() as ctx:
        def sb(name, shape, dt=fp32):
            return ctx.enter_context(nc.sbuf_tensor(name, shape, dt))

        def sem(name):
            return ctx.enter_context(nc.semaphore(name))

        def bank(name, dt=fp32):
            return ctx.enter_context(nc.psum_tensor(name, [P, 2048 // mybir.dt.size(dt)], dt))

        w1_sb = sb("w1_sb", [KS, D])
        w1_pick = sb("w1_pick", [KS, NPARTS])
        w1_hi = sb("w1_hi", [KS, D], bf16)
        w1_mid = sb("w1_mid", [KS, D], bf16)
        w1_r = sb("w1_r", [KS, D])
        w1_s = sb("w1_s", [KS, D], bf16)
        b1_sb = sb("b1_sb", [D, 1])
        w2_sb = sb("w2_sb", [D + 1, D])
        ws_sb = sb("ws_sb", [D + 2, D])
        wn_sb = sb("wn_sb", [D, D])
        x_sb = sb("x_sb", [NP, NC, D])
        h_sb = sb("h_sb", [NP, NC, D])
        tmp_n = sb("tmp_n", [NP, NC, D])
        stat = sb("stat", [NP, 4, NC])
        h_part = sb("h_part", [NP, NPARTS, NC, D], bf16)
        hT = sb("hT", [D + 2, NC, NP])
        self_sb = sb("self_sb", [NP, NC, D])
        aggT = sb("aggT", [D, AGGW])
        dst_sb = sb("dst_sb", [P, TPAD], i32)
        dstf = sb("dstf", [P, TPAD])
        local = sb("local", [P, TPAD])
        off = sb("off", [P, TPAD])
        base_b = sb("base_b", [P, BPAD])
        base_i = sb("base_i", [1, BPAD], i32)
        outside = sb("outside", [P, 2])
        misfits = sb("misfits", [1, 1], i32)
        iota_i = sb("iota_i", [P, SWEEP], i32)
        iota_f = sb("iota_f", [P, SWEEP])
        diff = sb("diff", [P, P], i32)
        first_i = sb("first_i", [P, 1], i32)
        first = sb("first", [P, 1])
        ident = sb("ident", [P, P])
        ident_b = sb("ident_b", [P, P], bf16)
        ones = sb("ones", [P, P])
        eps = sb("eps", [P, 1])
        idx_sb = [sb(f"idx{k}", [P, HTILES], i32) for k in range(2)]
        srcb = [sb(f"srcb{k}", [NP, PEG * TILE], i32) for k in range(2)]
        srcx = sb("srcx", [NP, PEG * TILE], fp16)
        pick = [sb(f"pick{k}", [NP, NC, PEG * TILE], bf16) for k in range(2)]
        nat = [sb(f"nat{k}", [P, HTILES, ED]) for k in range(2)]
        nat_r = sb("nat_r", [P, HTILES, ED])
        stack = [sb(f"stack{k}", [P, HTILES, KS], bf16) for k in range(2)]
        g_sb = [sb(f"gathered{k}", [P, HTILES, D]) for k in range(2)]
        stackT = [sb(f"stackT{k}", [KS, BLOCK * TILE], bf16) for k in range(2)]
        r_sb = [sb(f"relu{k}", [D + 1, BLOCK * TILE]) for k in range(2)]
        msg = [sb(f"msg{k}", [P, BLOCK, D]) for k in range(2)]
        msg_r = sb("msg_r", [P, BLOCK, D])
        part = [sb(f"part{k}", [P, NPARTS, BLOCK, D], bf16) for k in range(2)]
        hot = [sb(f"hot{k}", [P, BLOCK, WIN], bf16) for k in range(2)]
        idx_one = sb("idx_one", [P, 1], i32)
        dst_one = sb("dst_one", [P, 1])
        nat_one = sb("nat_one", [P, ED])
        natT_one = sb("natT_one", [ED, TILE])
        hot_sweep = sb("hot_sweep", [P, SWEEP])

        ps_t = bank("ps_t", bf16)
        ps_l1 = [bank(f"ps_l1{k}") for k in range(2)]
        ps_l2 = [bank(f"ps_l2{k}") for k in range(2)]
        ps_ag = bank("ps_ag")
        ps_g = [bank(f"ps_g{k}") for k in range(2)]

        x_in, w_in, dst_in, h_out, stored = (sem(n) for n in ("x_in", "w_in", "dst_in", "h_out", "stored"))
        v_step, a_step = sem("v_step"), sem("a_step")
        ones_set, iota_set, agg_zero, const_rows, idents = (
            sem(n) for n in ("ones_set", "iota_set", "agg_zero", "const_rows", "idents"))
        var_done, std_done, h_ready, hhi_done, hr_done, hmid_done, h_parts = (
            sem(n) for n in ("var_done", "std_done", "h_ready", "hhi_done", "hr_done", "hmid_done", "h_parts"))
        whi_done, wr_done, wmid_done, w1_ready = (sem(n) for n in ("whi_done", "wr_done", "wmid_done", "w1_ready"))
        dstf_ready, base_ps, outside_ready, count_ps, flag_ready = (
            sem(n) for n in ("dstf_ready", "base_ps", "outside_ready", "count_ps", "flag_ready"))
        ht_ps, ht_sb, self_ps, self_done = (sem(n) for n in ("ht_ps", "ht_sb", "self_ps", "self_done"))
        idx_in = [sem(f"idx_in{k}") for k in range(2)]
        srcb_in = [sem(f"srcb_in{k}") for k in range(2)]
        nat_in = [sem(f"nat_in{k}") for k in range(2)]
        srcx_done, pick_done, ahi_done, ar_done, amid_done, stack_done = (
            sem(n) for n in ("srcx_done", "pick_done", "ahi_done", "ar_done", "amid_done", "stack_done"))
        gathered = [sem(f"gathered_in{s}") for s in range(UNIT)]
        t_done, copy_done, l1_done, relu_done, l2_done, msg_done, hi_done, r_done, mid_done, lo_done = (
            sem(n) for n in ("t_done", "copy_done", "l1_done", "relu_done", "l2_done", "msg_done", "hi_done",
                             "r_done", "mid_done", "lo_done"))
        hot_done, scat_done, agg_done = (sem(n) for n in ("hot_done", "scat_done", "agg_done"))
        peg_done, evac_done = sem("peg_done"), sem("evac_done")
        out_ps, out_ready = sem("out_ps"), sem("out_ready")
        m_nat, m_idx, m_gather, m_t, m_copy, m_l1, m_relu, m_l2, m_msg, m_hot, m_scat, m_agg, m_dst, m_mask = (
            sem("m_" + n) for n in ("nat", "idx", "gather", "t", "copy", "l1", "relu", "l2", "msg", "hot", "scat",
                                    "agg", "dst", "mask"))
        block = ctx.enter_context(nc.Block())

        def known(i):
            return isinstance(i, int)

        def wait_count(eng, s, count):
            if not (known(count) and count < 1):
                eng.wait_ge(s, count)

        def flag_on(eng):
            eng.wait_ge(flag_ready, 1)
            return eng.value_load(misfits[0:1, 0:1], min_val=0, max_val=TPAD * TILE)

        @block.sync
        def _(sp):
            sp.dma_start(x_sb[0:112], x_v[0:112]).then_inc(x_in, 16)
            sp.dma_start(x_sb[112:NP], x_v[112:NP]).then_inc(x_in, 16)

            def load_half(u, k):
                h = 2 * u + k
                wait_count(sp, ar_done, h - 1)
                sp.dma_start(nat[k][:, :, :], attr[h]).then_inc(nat_in[k], 16)
                wait_count(sp, srcx_done, h - 1)
                sp.dma_start(srcb[k][:, :], src_rows[bass.ds(h * HTILES + SWG, PEG), :].rearrange("t e -> (t e)")
                             .unsqueeze(0).broadcast_to([NP, PEG * TILE])).then_inc(srcb_in[k], 16)
                wait_count(sp, msg_done, HALF * (h - 1))
                sp.dma_start(idx_sb[k][:, :], src[h]).then_inc(idx_in[k], 16)

            load_half(0, 0)
            load_half(0, 1)
            sp.wait_ge(h_ready, 1)
            sp.dma_start(h_v[0:112], h_sb[0:112]).then_inc(h_out, 16)
            sp.dma_start(h_v[112:NP], h_sb[112:NP]).then_inc(h_out, 16)
            with sp.Fori(1, UNITS) as u:
                load_half(u, 0)
                load_half(u, 1)
            load_half(UNITS, 0)
            with sp.If(flag_on(sp) > 0):
                def load_tile(t):
                    wait_count(sp, m_gather, 16 * t)
                    sp.dma_start(idx_one[:, :], src_rows[bass.ds(t, 1), :].rearrange("t p -> p t")
                                 ).then_inc(m_idx, 16)
                    wait_count(sp, m_t, t)
                    sp.dma_start(nat_one[:, :], attr_rows[bass.ds(t * TILE, TILE), :]).then_inc(m_nat, 16)

                load_tile(0)
                with sp.Fori(1, TILES) as t:
                    load_tile(t)
            for q in range(NQ):
                sp.wait_ge(out_ready, q + 1)
                sp.dma_start(out_v[:, 5 * q:5 * q + 5], h_sb[:, 5 * q:5 * q + 5]).then_inc(stored, 16)
            sp.wait_ge(stored, 16 * NQ)

        @block.gpsimd
        def _(pool):
            pool.memset(ones[:, :], 1.0).then_inc(ones_set, 1)
            pool.iota(diff[:, :], [[1, P]], base=0, channel_multiplier=-1).then_inc(iota_set, 1)
            pool.iota(first_i[:, :], [[1, 1]], base=0, channel_multiplier=NC).then_inc(iota_set, 1)
            pool.iota(iota_i[:, :], [[1, SWEEP]], base=0, channel_multiplier=0).then_inc(iota_set, 1)
            pool.memset(aggT[:, :], 0.0).then_inc(agg_zero, 1)

            def gather(u, k, tiles=SWG):
                pool.wait_ge(idx_in[k], 16 * u + 16)
                pool.nop(nofuse=True)
                for j in range(tiles):
                    pool.indirect_dma_start(
                        g_sb[k][:, j, :], None, h_dram[:, :],
                        bass.IndirectOffsetOnAxis(ap=idx_sb[k][:, j:j + 1], axis=0)
                    ).then_inc(gathered[HALF * k + j // BLOCK], 16)

            pool.wait_ge(h_out, 32)
            gather(0, 0)
            gather(0, 1)
            with pool.Fori(1, UNITS) as u:
                gather(u, 0)
                gather(u, 1)
            gather(UNITS, 0, TILES - UNITS * UNIT * BLOCK)
            with pool.If(flag_on(pool) > 0):
                pool.wait_ge(msg_done, BLOCKS)

                def gather_tile(t):
                    wait_count(pool, m_msg, t)
                    pool.wait_ge(m_idx, 16 * t + 16)
                    pool.nop(nofuse=True)
                    pool.indirect_dma_start(
                        g_sb[0][:, 0, :], None, h_dram[:, :],
                        bass.IndirectOffsetOnAxis(ap=idx_one[:, :], axis=0)).then_inc(m_gather, 16)

                gather_tile(0)
                with pool.Fori(1, TILES) as t:
                    gather_tile(t)

        @block.scalar
        def _(act):
            a = nc.scalar
            act.dma_start(dst_sb[:, :], dst).then_inc(dst_in, 16)
            for t, w in ((w1_sb, w1), (w1_pick, w1_part), (b1_sb, b1), (w2_sb, w2), (ws_sb, ws), (wn_sb, wn)):
                act.dma_start(t[:, :], w).then_inc(w_in, 16)
            act.wait_ge(w_in, 96)
            a.copy(w1_hi[:, :], w1_sb[:, :]).then_inc(whi_done, 1)
            act.wait_ge(var_done, 1)
            a.activation(stat[:, 2, :], stat[:, 1, :], ACT.Sqrt, bias=eps[0:NP, 0:1],
                         scale=1.0 / D).then_inc(std_done, 1)
            act.wait_ge(wr_done, 1)
            a.copy(w1_mid[:, :], w1_r[:, :]).then_inc(wmid_done, 1)

            def attr_hi(u, k):
                act.wait_ge(nat_in[k], 16 * u + 16)
                wait_count(act, t_done, HALF * (2 * u + k - 1))
                a.copy(stack[k][:, :, 0:3 * ED].rearrange("p t (n f) -> p t n f", n=3),
                       nat[k][:, :, :].unsqueeze(2).broadcast_to([P, HTILES, 3, ED])).then_inc(ahi_done, 1)

            def attr_mid(u, k):
                act.wait_ge(ar_done, 2 * u + k + 1)
                a.copy(stack[k][:, :, 3 * ED:6 * ED].rearrange("p t (n f) -> p t n f", n=3),
                       nat_r[:, :, :].unsqueeze(2).broadcast_to([P, HTILES, 3, ED])).then_inc(amid_done, 1)

            def copy_stack(u, s):
                b = UNIT * u + s
                act.wait_ge(t_done, b + 1)
                wait_count(act, l1_done, b - 1)
                a.copy(stackT[s % 2][:, :], ps_t[0:KS, 0:BLOCK * TILE]).then_inc(copy_done, 1)

            def relu(u, s):
                b = UNIT * u + s
                act.wait_ge(l1_done, b + 1)
                wait_count(act, l2_done, b - 1)
                a.activation(r_sb[s % 2][0:D, :], ps_l1[s % 2][0:D, :], ACT.Relu).then_inc(relu_done, 1)

            def msg_hi(u, s):
                b = UNIT * u + s
                act.wait_ge(msg_done, b + 1)
                wait_count(act, scat_done, b - 1)
                a.copy(part[s % 2][:, 0], msg[s % 2][:, :, :]).then_inc(hi_done, 1)

            def msg_mid(u, s):
                act.wait_ge(r_done, UNIT * u + s + 1)
                a.copy(part[s % 2][:, 1], msg_r[:, :, :]).then_inc(mid_done, 1)

            def evacuate(u, k, j):
                h = 2 * u + k
                act.wait_ge(peg_done, PEG * h + j + 1)
                wait_count(act, msg_done, HALF * (h - 1))
                a.copy(g_sb[k][:, SWG + j, :], ps_g[j][:, 0:D]).then_inc(evac_done, 1)

            def turn(u, s, last=False):
                k, q = s // HALF, s % HALF
                pu, ps = (u, s - 1) if s else (u - 1, UNIT - 1)
                before = not (known(u) and UNIT * u + s == 0)
                if q == 0 and before:
                    evacuate(*((u, 0) if k else (u - 1, 1)), 1)
                if not last or s + 1 < REST:
                    copy_stack(*((u, s + 1) if s + 1 < UNIT else (u + 1, 0)))
                relu(u, s)
                if before:
                    msg_hi(pu, ps)
                if q == 0 and not last:
                    attr_hi(*((u + 1, 0) if k else (u, 1)))
                if before:
                    msg_mid(pu, ps)
                if q == 1 and not last:
                    attr_mid(*((u + 1, 0) if k else (u, 1)))
                if q == 2 and not last:
                    evacuate(u, k, 0)

            attr_hi(0, 0)
            attr_mid(0, 0)
            act.wait_ge(h_ready, 1)
            a.copy(h_part[:, 0], h_sb[:, :, :]).then_inc(hhi_done, 1)
            for q in range(-(-NC // 4)):
                n = min(4, NC - 4 * q)
                act.wait_ge(ht_ps, q + 1)
                a.copy(hT[0:D, 4 * q:4 * q + n, :],
                       ps_g[q % 2][0:D, 0:n * NP].rearrange("p (c n) -> p c n", c=n)).then_inc(ht_sb, 1)
            act.wait_ge(hr_done, 1)
            a.copy(h_part[:, 1], tmp_n[:, :, :]).then_inc(hmid_done, 1)
            copy_stack(0, 0)
            for s in range(UNIT):
                turn(0, s)
            with act.Fori(1, UNITS) as u:
                for s in range(UNIT):
                    turn(u, s)
            for s in range(REST):
                turn(UNITS, s, last=True)
            msg_hi(UNITS, REST - 1)
            msg_mid(UNITS, REST - 1)
            with act.If(flag_on(act) > 0):
                def tile_step(t):
                    act.wait_ge(m_t, t + 1)
                    wait_count(act, m_l1, t)
                    a.copy(natT_one[:, :], ps_l1[1][0:ED, 0:TILE]).then_inc(m_copy, 1)
                    act.wait_ge(m_l1, t + 1)
                    wait_count(act, m_l2, t)
                    a.activation(r_sb[0][0:D, 0:TILE], ps_l1[0][0:D, 0:TILE], ACT.Relu,
                                 bias=b1_sb[:, 0:1]).then_inc(m_relu, 1)

                tile_step(0)
                with act.Fori(1, TILES) as t:
                    tile_step(t)

        @block.tensor
        def _(pe):
            mm = nc.tensor.matmul
            pe.wait_ge(ones_set, 1)
            pe.wait_ge(dstf_ready, 1)
            mm(ps_l2[0][:, 0:BPAD], ones[0:1, :], dstf[0:1, 0:TPAD:BLOCK], start=True, stop=True).then_inc(base_ps, 1)
            pe.wait_ge(outside_ready, 1)
            for k in range(2):
                last = mm(ps_l2[1][0:1, 0:1], outside[:, k:k + 1], ones[:, 0:1], start=(k == 0), stop=(k == 1))
            last.then_inc(count_ps, 1)
            pe.wait_ge(const_rows, 5)
            pe.wait_ge(idents, 2)
            pe.wait_ge(h_ready, 1)
            for q in range(-(-NC // 4)):
                if q >= 2:
                    pe.wait_ge(ht_sb, q - 1)
                for c in range(min(4, NC - 4 * q)):
                    last = nc.tensor.transpose(ps_g[q % 2][0:D, c * NP:(c + 1) * NP], h_sb[:, 4 * q + c, :],
                                               ident[0:NP, 0:NP])
                last.then_inc(ht_ps, 1)
            pe.wait_ge(w_in, 96)
            pe.wait_ge(ht_sb, -(-NC // 4))
            for q in range(NQ):
                if q >= 2:
                    pe.wait_ge(self_done, q - 1)
                for c in range(5):
                    last = mm(ps_g[q % 2][0:NP, c * D:(c + 1) * D], hT[:, 5 * q + c, :], ws_sb[:, :],
                              start=True, stop=True)
                last.then_inc(self_ps, 1)
            pe.wait_ge(flag_ready, 1)
            pe.wait_ge(w1_ready, 1)
            pe.wait_ge(h_parts, 1)
            pe.wait_ge(self_done, NQ)

            def transpose(u, s):
                b = UNIT * u + s
                if s % HALF == 0:
                    pe.wait_ge(stack_done, 2 * u + s // HALF + 1)
                wait_count(pe, copy_done, b)
                for j in range(BLOCK):
                    last = nc.tensor.transpose(ps_t[0:KS, j * TILE:(j + 1) * TILE],
                                               stack[s // HALF][:, (s % HALF) * BLOCK + j, :], ident_b[:, :])
                last.then_inc(t_done, 1)

            def layer1(u, s):
                b = UNIT * u + s
                pe.wait_ge(copy_done, b + 1)
                wait_count(pe, relu_done, b - 1)
                mm(ps_l1[s % 2][0:D, :], w1_s[:, :], stackT[s % 2][:, :], start=True, stop=True).then_inc(l1_done, 1)

            def layer2(u, s):
                b = UNIT * u + s
                pe.wait_ge(relu_done, b + 1)
                wait_count(pe, msg_done, b - 1)
                for j in range(BLOCK):
                    last = mm(ps_l2[s % 2][:, j * D:(j + 1) * D], r_sb[s % 2][:, j * TILE:(j + 1) * TILE],
                              w2_sb[:, :], start=True, stop=True)
                last.then_inc(l2_done, 1)

            def scatter(u, s):
                b = UNIT * u + s
                pe.wait_ge(lo_done, b + 1)
                pe.wait_ge(hot_done, b + 1)
                wait_count(pe, agg_done, b)
                for j in range(BLOCK):
                    for n in range(NPARTS):
                        last = mm(ps_ag[0:D, 0:WIN], part[s % 2][:, n, j, :], hot[s % 2][:, j, :],
                                  start=(j == 0 and n == 0), stop=(j == BLOCK - 1 and n == NPARTS - 1))
                last.then_inc(scat_done, 1)

            def gather(u, s):
                k, j, second = s // HALF, (s % HALF) // 2, s % 2
                h = 2 * u + k
                if s % HALF == 0:
                    pe.wait_ge(pick_done, h + 1)
                if not second:
                    wait_count(pe, evac_done, PEG * h + j - 1)
                for c in (range(NC // 2, NC) if second else range(NC // 2)):
                    for n in range(NPARTS):
                        last = mm(ps_g[j][:, 0:D], pick[k][:, c, j * TILE:(j + 1) * TILE], h_part[:, n, c, :],
                                  start=(c == 0 and n == 0), stop=(c == NC - 1 and n == NPARTS - 1))
                if second:
                    last.then_inc(peg_done, 1)

            def turn(u, s, last=False):
                if not last or s + 1 < REST:
                    transpose(*((u, s + 1) if s + 1 < UNIT else (u + 1, 0)))
                layer1(u, s)
                if not (known(u) and UNIT * u + s < 1):
                    layer2(*((u, s - 1) if s >= 1 else (u - 1, s + UNIT - 1)))
                if not (known(u) and UNIT * u + s < 2):
                    scatter(*((u, s - 2) if s >= 2 else (u - 1, s + UNIT - 2)))
                if not last:
                    gather(u, s)

            transpose(0, 0)
            for s in range(UNIT):
                turn(0, s)
            with pe.Fori(1, UNITS) as u:
                for s in range(UNIT):
                    turn(u, s)
            for s in range(REST):
                turn(UNITS, s, last=True)
            layer2(UNITS, REST - 1)
            scatter(UNITS, REST - 2)
            scatter(UNITS, REST - 1)
            with pe.If(flag_on(pe) > 0):
                pe.wait_ge(agg_done, BLOCKS)

                def tile_step(t):
                    pe.wait_ge(m_nat, 16 * t + 16)
                    wait_count(pe, m_copy, t)
                    nc.tensor.transpose(ps_l1[1][0:ED, 0:TILE], nat_one[:, :], ident[:, :]).then_inc(m_t, 1)
                    pe.wait_ge(m_copy, t + 1)
                    wait_count(pe, m_relu, t)
                    mm(ps_l1[0][0:D, 0:TILE], w1_sb[0:ED, :], natT_one[:, :], start=True, stop=True).then_inc(m_l1, 1)
                    pe.wait_ge(m_relu, t + 1)
                    wait_count(pe, m_msg, t)
                    mm(ps_l2[0][:, 0:D], r_sb[0][:, 0:TILE], w2_sb[:, :], start=True, stop=True).then_inc(m_l2, 1)
                    pe.wait_ge(m_msg, t + 1)
                    for w in range(SWEEPS):
                        pe.wait_ge(m_hot, SWEEPS * t + w + 1)
                        wait_count(pe, m_agg, SWEEPS * t + w)
                        mm(ps_ag[0:D, :], msg[0][:, 0, :], hot_sweep[:, :], start=True, stop=True).then_inc(m_scat, 1)

                tile_step(0)
                with pe.Fori(1, TILES) as t:
                    tile_step(t)
                pe.wait_ge(m_agg, SWEEPS * TILES)
            pe.wait_ge(agg_done, BLOCKS)
            for q in range(NQ):
                if q >= 2:
                    pe.wait_ge(out_ready, q - 1)
                for c in range(5):
                    last = mm(ps_g[q % 2][0:NP, c * D:(c + 1) * D], aggT[:, 5 * q + c:N:NC], wn_sb[:, :],
                              start=True, stop=True)
                last.then_inc(out_ps, 1)

        @block.vector
        def _(dve):
            v = nc.vector
            steps = [0]

            def step(ins):
                steps[0] += 1
                ins.then_inc(v_step, 1)
                dve.wait_ge(v_step, steps[0])

            def per_node(a):
                return a.unsqueeze(2).broadcast_to([NP, NC, D])

            v.memset(eps[:, :], 1e-5)
            v.memset(hT[D:D + 2, :, :], 1.0).then_inc(const_rows, 1)
            for k in range(2):
                v.memset(r_sb[k][D:D + 1, :], 1.0).then_inc(const_rows, 1)
                v.memset(stack[k][:, :, KA:KS], 1.0).then_inc(const_rows, 1)
            dve.wait_ge(x_in, 32)
            step(v.tensor_reduce(stat[:, 0, :], x_sb[:, :, :], AX.X, ALU.add))
            step(v.tensor_scalar(stat[:, 0, :], stat[:, 0, :], 1.0 / D, None, ALU.mult))
            step(v.tensor_tensor(h_sb[:, :, :], x_sb[:, :, :], per_node(stat[:, 0, :]), ALU.subtract))
            step(v.tensor_tensor(tmp_n[:, :, :], h_sb[:, :, :], h_sb[:, :, :], ALU.mult))
            v.tensor_reduce(stat[:, 1, :], tmp_n[:, :, :], AX.X, ALU.add).then_inc(var_done, 1)
            dve.wait_ge(std_done, 1)
            step(v.reciprocal(stat[:, 3, :], stat[:, 2, :]))
            step(v.tensor_tensor(tmp_n[:, :, :], h_sb[:, :, :], per_node(stat[:, 3, :]), ALU.mult))
            v.tensor_scalar(h_sb[:, :, :], tmp_n[:, :, :], 0.0, None, ALU.max).then_inc(h_ready, 1)
            dve.wait_ge(iota_set, 3)
            v.tensor_scalar(ident[:, :], diff[:, :], 0.0, None, ALU.is_equal).then_inc(idents, 1)
            v.tensor_scalar(ident_b[:, :], diff[:, :], 0.0, None, ALU.is_equal).then_inc(idents, 1)
            v.tensor_copy(first[:, :], first_i[:, :])
            v.tensor_copy(iota_f[:, :], iota_i[:, :])

            dve.wait_ge(dst_in, 16)
            v.tensor_copy(dstf[:, :], dst_sb[:, :]).then_inc(dstf_ready, 1)
            dve.wait_ge(base_ps, 1)
            step(v.tensor_scalar(base_b[:, :], ps_l2[0][:, 0:BPAD], 0.0, None, ALU.max))
            step(v.tensor_copy(base_i[:, :], base_b[0:1, :]))
            step(v.tensor_tensor(local[:, :].rearrange("p (g j) -> p g j", j=BLOCK),
                                 dstf[:, :].rearrange("p (g j) -> p g j", j=BLOCK),
                                 base_b[:, :].unsqueeze(2).broadcast_to([P, BPAD, BLOCK]), ALU.subtract))
            step(v.tensor_scalar(off[:, :], local[:, :], float(WIN), 0.0, ALU.is_ge, ALU.add,
                                 accum_out=outside[:, 0:1]))
            v.tensor_scalar(off[:, :], local[:, :], 0.0, 0.0, ALU.is_lt, ALU.add,
                            accum_out=outside[:, 1:2]).then_inc(outside_ready, 1)
            dve.wait_ge(count_ps, 1)
            v.tensor_scalar(misfits[:, :], ps_l2[1][0:1, 0:1], float(-PADS), None, ALU.add).then_inc(flag_ready, 1)
            dve.wait_ge(whi_done, 1)
            v.tensor_tensor(w1_r[:, :], w1_sb[:, :], w1_hi[:, :], ALU.subtract).then_inc(wr_done, 1)

            def attr_r(u, k):
                h = 2 * u + k
                dve.wait_ge(ahi_done, h + 1)
                wait_count(dve, amid_done, h)
                v.tensor_tensor(nat_r[:, :, :], nat[k][:, :, :], stack[k][:, :, 0:ED],
                                ALU.subtract).then_inc(ar_done, 1)

            def attr_lo(u, k):
                h = 2 * u + k
                dve.wait_ge(amid_done, h + 1)
                v.tensor_tensor(stack[k][:, :, 6 * ED:7 * ED], nat_r[:, :, :], stack[k][:, :, 3 * ED:4 * ED],
                                ALU.subtract).then_inc(stack_done, 1)

            def src_offsets(u, k):
                h = 2 * u + k
                dve.wait_ge(srcb_in[k], 16 * u + 16)
                v.tensor_scalar(srcx[:, :], srcb[k][:, :], first[0:NP, 0:1], None,
                                ALU.subtract).then_inc(srcx_done, 1)
                dve.wait_ge(srcx_done, h + 1)

            def picks(u, k, q):
                h = 2 * u + k
                if q == 0:
                    wait_count(dve, peg_done, PEG * (h - 1))
                for c in range(NC * q // HALF, NC * (q + 1) // HALF):
                    last = v.tensor_scalar(pick[k][:, c, :], srcx[:, :], float(c), None, ALU.is_equal)
                if q == HALF - 1:
                    last.then_inc(pick_done, 1)

            def message(u, s):
                b, k, q = UNIT * u + s, s // HALF, s % HALF
                dve.wait_ge(l2_done, b + 1)
                full = 16 * (SWG % BLOCK or BLOCK) if q == HALF - 1 else 16 * BLOCK
                mine = full if not (known(u) and u == UNITS) else \
                    16 * min(BLOCK, TILES - (UNITS * UNIT + s) * BLOCK)
                dve.wait_ge(gathered[s], full * u + mine)
                if q == HALF - 1:
                    dve.wait_ge(evac_done, PEG * (2 * u + k + 1))
                wait_count(dve, hi_done, b - 1)
                v.tensor_tensor(msg[s % 2][:, :, :],
                                ps_l2[s % 2][:, 0:BLOCK * D].rearrange("p (j f) -> p j f", j=BLOCK),
                                g_sb[k][:, q * BLOCK:(q + 1) * BLOCK, :], ALU.mult).then_inc(msg_done, 1)

            def msg_rest(u, s):
                b = UNIT * u + s
                dve.wait_ge(hi_done, b + 1)
                wait_count(dve, mid_done, b)
                v.tensor_tensor(msg_r[:, :, :], msg[s % 2][:, :, :], part[s % 2][:, 0],
                                ALU.subtract).then_inc(r_done, 1)

            def msg_lo(u, s):
                b = UNIT * u + s
                dve.wait_ge(mid_done, b + 1)
                v.tensor_tensor(part[s % 2][:, 2], msg_r[:, :, :], part[s % 2][:, 1],
                                ALU.subtract).then_inc(lo_done, 1)

            def one_hot(u, s):
                b = UNIT * u + s
                wait_count(dve, scat_done, b - 1)
                v.tensor_tensor(hot[s % 2][:, :, :],
                                local[:, bass.ds(b * BLOCK, BLOCK)].unsqueeze(2).broadcast_to([P, BLOCK, WIN]),
                                iota_f[:, 0:WIN].unsqueeze(1).broadcast_to([P, BLOCK, WIN]),
                                ALU.is_equal).then_inc(hot_done, 1)

            def aggregate(u, s):
                b = UNIT * u + s
                at = dve.value_load(base_i[0:1, bass.ds(b, 1)], min_val=0, max_val=N - 1)
                dve.wait_ge(scat_done, b + 1)
                wait_count(dve, agg_done, b)
                win = aggT[:, bass.ds(at, WIN)]
                v.tensor_tensor(win, win, ps_ag[0:D, 0:WIN], ALU.add).then_inc(agg_done, 1)

            def turn(u, s, last=False):
                q = s % HALF
                nu, nk = (u, 1) if s < HALF else (u + 1, 0)
                pu, ps = (u, s - 1) if s else (u - 1, UNIT - 1)
                qu, qs = (u, s - 2) if s >= 2 else (u - 1, s + UNIT - 2)
                before = not (known(u) and UNIT * u + s == 0)
                more = not last and not (known(u) and u == UNITS)
                if before:
                    message(pu, ps)
                if q == 0 and more:
                    src_offsets(nu, nk)
                if q == 1 and more:
                    attr_r(nu, nk)
                if q == 2 and more:
                    attr_lo(nu, nk)
                if before:
                    one_hot(pu, ps)
                if more:
                    picks(nu, nk, q)
                if before:
                    msg_rest(pu, ps)
                if not (known(u) and UNIT * u + s < 2):
                    aggregate(qu, qs)
                if before:
                    msg_lo(pu, ps)

            attr_r(0, 0)
            dve.wait_ge(wmid_done, 1)
            step(v.tensor_tensor(w1_r[:, :], w1_r[:, :], w1_mid[:, :], ALU.subtract))
            step(v.tensor_scalar(w1_r[:, :], w1_r[:, :], w1_pick[:, 2:3], None, ALU.mult))
            step(v.scalar_tensor_tensor(w1_r[:, :], w1_mid[:, :], w1_pick[:, 1:2], w1_r[:, :], ALU.mult, ALU.add))
            v.scalar_tensor_tensor(w1_s[:, :], w1_hi[:, :], w1_pick[:, 0:1], w1_r[:, :], ALU.mult,
                                   ALU.add).then_inc(w1_ready, 1)
            attr_lo(0, 0)
            dve.wait_ge(hhi_done, 1)
            v.tensor_tensor(tmp_n[:, :, :], h_sb[:, :, :], h_part[:, 0], ALU.subtract).then_inc(hr_done, 1)
            src_offsets(0, 0)
            for q in range(HALF):
                picks(0, 0, q)
            for q in range(NQ):
                dve.wait_ge(self_ps, q + 1)
                v.tensor_copy(self_sb[:, 5 * q:5 * q + 5, :],
                              ps_g[q % 2][0:NP, 0:5 * D].rearrange("p (c f) -> p c f", c=5)).then_inc(self_done, 1)
            dve.wait_ge(hmid_done, 1)
            v.tensor_tensor(h_part[:, 2], tmp_n[:, :, :], h_part[:, 1], ALU.subtract).then_inc(h_parts, 1)
            dve.wait_ge(agg_zero, 1)
            for s in range(UNIT):
                turn(0, s)
            with dve.Fori(1, UNITS) as u:
                for s in range(UNIT):
                    turn(u, s)
            for s in range(REST):
                turn(UNITS, s, last=True)
            message(UNITS, REST - 1)
            one_hot(UNITS, REST - 1)
            msg_rest(UNITS, REST - 1)
            aggregate(UNITS, REST - 2)
            msg_lo(UNITS, REST - 1)
            aggregate(UNITS, REST - 1)
            with dve.If(flag_on(dve) > 0):
                dve.wait_ge(agg_done, BLOCKS)
                masks = [0]

                def mask(ins):
                    masks[0] += 1
                    ins.then_inc(m_mask, 1)
                    dve.wait_ge(m_mask, masks[0])

                mask(v.tensor_scalar(off[:, :], local[:, :], 0.0, None, ALU.is_ge))
                mask(v.scalar_tensor_tensor(off[:, :], local[:, :], float(WIN), off[:, :], ALU.is_lt, ALU.mult))
                mask(v.tensor_scalar(local[:, :], dstf[:, :], 1.0, None, ALU.add))
                mask(v.tensor_tensor(off[:, :], off[:, :], local[:, :], ALU.mult))
                mask(v.tensor_tensor(dstf[:, :], dstf[:, :], off[:, :], ALU.subtract))

                def tile_step(t):
                    v.tensor_copy(dst_one[:, :], dstf[:, bass.ds(t, 1)]).then_inc(m_dst, 1)
                    dve.wait_ge(m_l2, t + 1)
                    dve.wait_ge(m_gather, 16 * t + 16)
                    wait_count(dve, m_scat, SWEEPS * t)
                    v.tensor_tensor(msg[0][:, 0, :], ps_l2[0][:, 0:D], g_sb[0][:, 0, :],
                                    ALU.mult).then_inc(m_msg, 1)
                    dve.wait_ge(m_dst, t + 1)
                    for w in range(SWEEPS):
                        wait_count(dve, m_scat, SWEEPS * t + w)
                        v.tensor_scalar(hot_sweep[:, :], iota_f[:, :], dst_one[:, 0:1], float(-w * SWEEP),
                                        ALU.subtract, ALU.is_equal).then_inc(m_hot, 1)
                        dve.wait_ge(m_scat, SWEEPS * t + w + 1)
                        wait_count(dve, m_agg, SWEEPS * t + w)
                        win = aggT[:, w * SWEEP:(w + 1) * SWEEP]
                        v.tensor_tensor(win, win, ps_ag[0:D, :], ALU.add).then_inc(m_agg, 1)

                tile_step(0)
                with dve.Fori(1, TILES) as t:
                    tile_step(t)
            for q in range(NQ):
                dve.wait_ge(out_ps, q + 1)
                cs = slice(5 * q, 5 * q + 5)
                step(v.tensor_tensor(tmp_n[:, cs, :], self_sb[:, cs, :],
                                     ps_g[q % 2][0:NP, 0:5 * D].rearrange("p (c f) -> p c f", c=5), ALU.add))
                v.scalar_tensor_tensor(h_sb[:, cs, :], tmp_n[:, cs, :], 0.0, x_sb[:, cs, :],
                                       ALU.max, ALU.add).then_inc(out_ready, 1)


def kernel(x, src, dst, edge_attr_17, L0_gnn_W1, L0_gnn_b1, L0_gnn_W2, L0_gnn_b2, L0_gnn_Ws, L0_gnn_bs,
           L0_gnn_Wn, L0_gnn_bn):
    import numpy as np
    import concourse.bacc as bacc
    from concourse.bass_utils import run_bass_kernel_spmd

    def padded(a, fill):
        a = np.asarray(a)
        return np.concatenate([a, np.full((PADS, *a.shape[1:]), fill, a.dtype)])

    def by_half(a, fill):
        a = padded(a, fill)
        return np.ascontiguousarray(a.reshape(HALVES, HTILES, TILE, *a.shape[1:]).swapaxes(1, 2))

    src_h, dst_h = by_half(src, 0), by_half(dst, -1)
    b1, b2, bs, bn = (np.asarray(b)[None, :] for b in (L0_gnn_b1, L0_gnn_b2, L0_gnn_bs, L0_gnn_bn))
    w1_t = np.asarray(L0_gnn_W1).T
    parts = np.concatenate([np.repeat(W_PART, ED), np.arange(NPARTS)])
    arrays = {
        "x_in": np.ascontiguousarray(x),
        "src_half": src_h,
        "src_rows": padded(src, 0).reshape(TPAD, TILE),
        "dst_tiles": np.ascontiguousarray(dst_h.swapaxes(0, 1).reshape(TILE, TPAD)),
        "attr_half": by_half(edge_attr_17, 0),
        "attr_rows": padded(edge_attr_17, 0),
        "w1_rows": np.concatenate([w1_t] * len(W_PART) + [b1] * NPARTS),
        "w1_part": (parts[:, None] == np.arange(NPARTS)[None, :]).astype(np.float32),
        "b1_col": np.ascontiguousarray(b1.T),
        "w2_t": np.concatenate([np.asarray(L0_gnn_W2).T, b2]),
        "ws_t": np.concatenate([np.asarray(L0_gnn_Ws).T, bs, bn]),
        "wn_t": np.ascontiguousarray(np.asarray(L0_gnn_Wn).T),
    }
    nc = bacc.Bacc("TRN2", target_bir_lowering=False, num_devices=1)
    args = [nc.dram_tensor(n, a.shape, mybir.dt.from_np(a.dtype), kind="ExternalInput").ap()
            for n, a in arrays.items()]
    out = nc.dram_tensor("out_rows", [N, D], mybir.dt.float32, kind="ExternalOutput").ap()
    gnn_layer(nc, *args, out)
    r = run_bass_kernel_spmd(nc, [arrays], core_ids=[0])
    return r.results[0]["out_rows"]
```

```python
import concourse.bass as bass
from concourse import mybir
from contextlib import ExitStack

N, D, ED, E = 3125, 96, 17, 103125
P = 128
TILE = P
BLOCK = 4
HALF = 4
HTILES = BLOCK * HALF
UNIT = 2 * HALF
TILES = -(-E // TILE)
BLOCKS = -(-TILES // BLOCK)
UNITS = BLOCKS // UNIT
REST = BLOCKS - UNITS * UNIT
HALVES = -(-BLOCKS // HALF)
TPAD = HALVES * HTILES
PADS = TPAD * TILE - E
BPAD = HALVES * HALF
PEG = (2, 2)
UPEG = sum(PEG)
PMAX = max(PEG)
WIN = 32
SWEEP = 512
SWEEPS = -(-N // SWEEP)
AGGW = SWEEPS * SWEEP
NP = 125
NC = N // NP
NQ = NC // 5
CHUNKS = [(0, 9), (9, 17), (17, NC)]
SHARES = [(5, 3, 1), (3, 4, 1), (4, 3, 1)]
assert [sum(n) for n in SHARES] == [c1 - c0 for c0, c1 in CHUNKS]
NPARTS = 3
A_PART = [0, 0, 0, 1, 1, 1, 2]
W_PART = [0, 1, 2, 0, 1, 2, 0]
KA = len(A_PART) * ED
KS = KA + NPARTS
assert AGGW >= N + WIN and KS <= P and 0 < REST <= HALF and TILES - UNITS * UNIT * BLOCK <= HTILES - PMAX
PICKS = PMAX * TILE
PICKS_LATE = 3


def peg_before(u, k):
    return UPEG * u + (0 if k else -PEG[0])


def peg_slices(k):
    work = [(j, c) for j in range(PEG[k]) for c in range(NC)]
    return [work[q * len(work) // HALF:(q + 1) * len(work) // HALF] for q in range(HALF)]


def peg_ends(k, q):
    return [j for j, c in peg_slices(k)[q] if c == NC - 1]


def peg_bank(k, j):
    return (j + k * PEG[0]) % 2


def peg_reuse(k, j):
    order = [peg_bank(a, b) for a in range(2) for b in range(PEG[a])] * 2
    at = UPEG + j + k * PEG[0]
    return next(d for d in range(1, at) if order[at - d] == order[at])


def gnn_layer(nc, x, src, src_rows, dst, attr, attr_rows, w1, w1_part, b1, w2, ws, wn, out):
    fp32, bf16, fp16, i32 = (mybir.dt.float32, mybir.dt.bfloat16, mybir.dt.float16, mybir.dt.int32)
    ALU = mybir.AluOpType
    ACT = mybir.ActivationFunctionType
    AX = mybir.AxisListType

    x_v = x.rearrange("(p c) f -> p c f", p=NP)
    out_v = out.rearrange("(p c) f -> p c f", p=NP)
    h_dram = nc.dram_tensor("h_rows", [N, D], fp32, kind="Internal").ap()
    h_v = h_dram.rearrange("(p c) f -> p c f", p=NP)

    with ExitStack() as ctx:
        def sb(name, shape, dt=fp32):
            return ctx.enter_context(nc.sbuf_tensor(name, shape, dt))

        def sem(name):
            return ctx.enter_context(nc.semaphore(name))

        def bank(name, dt=fp32):
            return ctx.enter_context(nc.psum_tensor(name, [P, 2048 // mybir.dt.size(dt)], dt))

        w1_sb = sb("w1_sb", [KS, D])
        w1_pick = sb("w1_pick", [KS, NPARTS])
        w1_hi = sb("w1_hi", [KS, D], bf16)
        w1_mid = sb("w1_mid", [KS, D], bf16)
        w1_r = sb("w1_r", [KS, D])
        w1_s = sb("w1_s", [KS, D], bf16)
        b1_sb = sb("b1_sb", [D, 1])
        w2_sb = sb("w2_sb", [D + 1, D])
        ws_sb = sb("ws_sb", [D + 2, D])
        wn_sb = sb("wn_sb", [D, D])
        x_sb = sb("x_sb", [NP, NC, D])
        h_sb = sb("h_sb", [NP, NC, D])
        tmp_n = sb("tmp_n", [NP, NC, D])
        stats = sb("stats", [NP, NC, 6])
        stat = sb("stat", [NP, 6, NC])
        h_part = sb("h_part", [NP, NC, NPARTS, D], bf16)
        hT = sb("hT", [D + 2, NC, NP])
        aggT = sb("aggT", [D, AGGW])
        dst_sb = sb("dst_sb", [P, TPAD], i32)
        dstf = sb("dstf", [P, TPAD])
        local = sb("local", [P, TPAD])
        off = sb("off", [P, TPAD])
        base_b = sb("base_b", [P, BPAD])
        base_i = sb("base_i", [1, BPAD], i32)
        outside = sb("outside", [P, 2])
        misfits = sb("misfits", [1, 1], i32)
        iota_i = sb("iota_i", [P, SWEEP], i32)
        iota_f = sb("iota_f", [P, SWEEP])
        diff = sb("diff", [P, P], i32)
        first_i = sb("first_i", [P, 1], i32)
        first = sb("first", [P, 1])
        ident = sb("ident", [P, P])
        ident_b = sb("ident_b", [P, P], bf16)
        ones = sb("ones", [P, P])
        eps = sb("eps", [P, 2])
        idx_sb = [sb(f"idx{k}", [P, HTILES], i32) for k in range(2)]
        srcb = [sb(f"srcb{k}", [NP, PICKS], i32) for k in range(2)]
        srcx = [sb(f"srcx{k}", [NP, PICKS], fp16) for k in range(2)]
        pick = [sb(f"pick{k}", [NP, NC, PICKS], bf16) for k in range(2)]
        nat = [sb(f"nat{k}", [P, HTILES, ED]) for k in range(2)]
        nat_r = sb("nat_r", [P, HTILES, ED])
        stack = [sb(f"stack{k}", [P, HTILES, KS], bf16) for k in range(2)]
        g_sb = [sb(f"gathered{k}", [P, HTILES, D]) for k in range(2)]
        stackT = [sb(f"stackT{k}", [KS, BLOCK * TILE], bf16) for k in range(2)]
        r_sb = [sb(f"relu{k}", [D + 1, BLOCK * TILE]) for k in range(2)]
        msg = [sb(f"msg{k}", [P, BLOCK, D]) for k in range(2)]
        hot = [sb(f"hot{k}", [P, BLOCK, WIN]) for k in range(2)]
        idx_one = sb("idx_one", [P, 1], i32)
        dst_one = sb("dst_one", [P, 1])
        nat_one = sb("nat_one", [P, ED])
        natT_one = sb("natT_one", [ED, TILE])
        hot_sweep = sb("hot_sweep", [P, SWEEP])

        ps_t = bank("ps_t", bf16)
        ps_l1 = [bank(f"ps_l1{k}") for k in range(2)]
        ps_l2 = [bank(f"ps_l2{k}") for k in range(2)]
        ps_ag = bank("ps_ag")
        ps_g = [bank(f"ps_g{k}") for k in range(2)]

        x_in = [sem(f"x_in{q}") for q in range(len(CHUNKS))]
        w_in, dst_in, h_out, stored = (sem(n) for n in ("w_in", "dst_in", "h_out", "stored"))
        v_step, p_step = sem("v_step"), sem("p_step")
        ones_set, iota_set, agg_zero, const_rows, idents = (
            sem(n) for n in ("ones_set", "iota_set", "agg_zero", "const_rows", "idents"))
        var_done, std_done, scale_done, mean_done, shift_done = (
            sem(n) for n in ("var_done", "std_done", "scale_done", "mean_done", "shift_done"))
        hhi_done, hr_done, hmid_done, h_parts = (sem(n) for n in ("hhi_done", "hr_done", "hmid_done", "h_parts"))
        whi_done, wr_done, wmid_done, w1_ready = (sem(n) for n in ("whi_done", "wr_done", "wmid_done", "w1_ready"))
        h_dve, h_act, h_pool = (sem(n) for n in ("h_dve", "h_act", "h_pool"))
        base_read, own_rows, eps_set = sem("base_read"), sem("own_rows"), sem("eps_set")
        dstf_ready, base_ps, outside_ready, count_ps, flag_ready = (
            sem(n) for n in ("dstf_ready", "base_ps", "outside_ready", "count_ps", "flag_ready"))
        node_ps, node_sb = sem("node_ps"), sem("node_sb")
        idx_in = [sem(f"idx_in{k}") for k in range(2)]
        srcb_in = [sem(f"srcb_in{k}") for k in range(2)]
        nat_in = [sem(f"nat_in{k}") for k in range(2)]
        srcx_done, pick_done, ahi_done, ar_done, amid_done, stack_done = (
            sem(n) for n in ("srcx_done", "pick_done", "ahi_done", "ar_done", "amid_done", "stack_done"))
        gathered = [sem(f"gathered_in{s}") for s in range(UNIT)]
        t_done, copy_done, l1_done, relu_done, l2_done, msg_done = (
            sem(n) for n in ("t_done", "copy_done", "l1_done", "relu_done", "l2_done", "msg_done"))
        hot_done, scat_done, agg_done = (sem(n) for n in ("hot_done", "scat_done", "agg_done"))
        peg_done, evac_done = sem("peg_done"), sem("evac_done")
        out_ps, out_ready = sem("out_ps"), sem("out_ready")
        m_nat, m_idx, m_gather, m_t, m_copy, m_l1, m_relu, m_l2, m_msg, m_hot, m_scat, m_agg, m_dst, m_mask = (
            sem("m_" + n) for n in ("nat", "idx", "gather", "t", "copy", "l1", "relu", "l2", "msg", "hot", "scat",
                                    "agg", "dst", "mask"))
        block = ctx.enter_context(nc.Block())

        def known(i):
            return isinstance(i, int)

        def wait_count(eng, s, count):
            if not (known(count) and count < 1):
                eng.wait_ge(s, count)

        def landed(u, s):
            if known(u) and u < 0:
                return 0
            k, q = s // HALF, s % HALF
            each = max(0, min(BLOCK, HTILES - PEG[k] - q * BLOCK))
            first = BLOCK if k == 0 else each
            if known(u) and u == UNITS:
                each_last = max(0, min(BLOCK, TILES - (UNITS * UNIT + s) * BLOCK))
                return 16 * (first + each * (UNITS - 1) + each_last)
            return 16 * first + 16 * each * u

        def flag_on(eng):
            eng.wait_ge(flag_ready, 1)
            return eng.value_load(misfits[0:1, 0:1], min_val=0, max_val=TPAD * TILE)

        NODE_TASKS = -(-NC // 4)
        assert NODE_TASKS <= 2 * HALF

        ps_count = ps_g[1 - peg_bank(1, 0)][0:1, 0:1]

        ps_out = [ps_g[0], ps_g[1], ps_l1[0], ps_l1[1], ps_l2[0]]
        assert len(ps_out) == NQ

        one_t = ps_l2[1][0:ED, 0:TILE]
        one_l1 = ps_l2[1][0:D, TILE:2 * TILE]
        one_l2 = ps_l2[1][:, 2 * TILE:2 * TILE + D]

        @block.sync
        def _(sp):
            for q, (c0, c1) in enumerate(CHUNKS):
                sp.dma_start(x_sb[0:112, c0:c1], x_v[0:112, c0:c1]).then_inc(x_in[q], 16)
                sp.dma_start(x_sb[112:NP, c0:c1], x_v[112:NP, c0:c1]).then_inc(x_in[q], 16)

            def load_half(u, k):
                h = 2 * u + k
                wait_count(sp, ar_done, h - 1)
                sp.dma_start(nat[k][:, :, :], attr[h]).then_inc(nat_in[k], 16)
                wait_count(sp, srcx_done, h - 1)
                if not (known(u) and h == 0):
                    last_tiles = src_rows[bass.ds(h * HTILES + HTILES - PMAX, PMAX), :]
                    sp.dma_start(srcb[k][:, :], last_tiles.rearrange("t e -> (t e)").unsqueeze(0)
                                 .broadcast_to([NP, PICKS])).then_inc(srcb_in[k], 16)
                for q in range(HALF):
                    wait_count(sp, gathered[HALF * k + q], landed(u - 1, HALF * k + q))
                    sp.nop(nofuse=True)
                sp.dma_start(idx_sb[k][:, :], src[h]).then_inc(idx_in[k], 16)

            sp.dma_start(dst_sb[:, :], dst).then_inc(dst_in, 16)
            load_half(0, 0)
            for t, w in ((w1_sb, w1), (w1_pick, w1_part), (b1_sb, b1), (w2_sb, w2), (ws_sb, ws), (wn_sb, wn)):
                sp.dma_start(t[:, :], w).then_inc(w_in, 16)
            load_half(0, 1)
            for q, (c0, c1) in enumerate(CHUNKS):
                for part in (h_dve, h_act, h_pool):
                    sp.wait_ge(part, q + 1)
                sp.dma_start(h_v[0:112, c0:c1], h_sb[0:112, c0:c1]).then_inc(h_out, 16)
                sp.dma_start(h_v[112:NP, c0:c1], h_sb[112:NP, c0:c1]).then_inc(h_out, 16)
            with sp.Fori(1, UNITS) as u:
                load_half(u, 0)
                load_half(u, 1)
            load_half(UNITS, 0)
            with sp.If(flag_on(sp) > 0):
                def load_tile(t):
                    wait_count(sp, m_gather, 16 * t)
                    sp.dma_start(idx_one[:, :], src_rows[bass.ds(t, 1), :].rearrange("t p -> p t")
                                 ).then_inc(m_idx, 16)
                    wait_count(sp, m_t, t)
                    sp.dma_start(nat_one[:, :], attr_rows[bass.ds(t * TILE, TILE), :]).then_inc(m_nat, 16)

                load_tile(0)
                with sp.Fori(1, TILES) as t:
                    load_tile(t)
            for q in range(NQ):
                sp.wait_ge(out_ready, q + 1)
                sp.dma_start(out_v[:, 5 * q:5 * q + 5], h_sb[:, 5 * q:5 * q + 5]).then_inc(stored, 16)
            sp.wait_ge(stored, 16 * NQ)

        @block.gpsimd
        def _(pool):
            pool.memset(ones[:, :], 1.0).then_inc(ones_set, 1)
            pool.iota(diff[:, :], [[1, P]], base=0, channel_multiplier=-1).then_inc(iota_set, 1)
            pool.iota(first_i[:, :], [[1, 1]], base=0, channel_multiplier=NC).then_inc(iota_set, 1)
            pool.iota(iota_i[:, :], [[1, SWEEP]], base=0, channel_multiplier=0).then_inc(iota_set, 1)
            pool.memset(aggT[:, :], 0.0).then_inc(agg_zero, 1)

            def gather(u, k, tiles):
                pool.wait_ge(idx_in[k], 16 * u + 16)
                wait_count(pool, msg_done, HALF * (2 * u + k - 1))
                pool.nop(nofuse=True)
                for j in range(tiles):
                    pool.indirect_dma_start(
                        g_sb[k][:, j, :], None, h_dram[:, :],
                        bass.IndirectOffsetOnAxis(ap=idx_sb[k][:, j:j + 1], axis=0)
                    ).then_inc(gathered[HALF * k + j // BLOCK], 16)

            pool.wait_ge(scale_done, 1)
            for q, (c0, c1) in enumerate(CHUNKS):
                p0 = c1 - SHARES[q][2]
                for c in range(p0, c1):
                    last = nc.gpsimd.tensor_scalar(tmp_n[:, c, :], x_sb[:, c, :], stat[:, 1, c:c + 1],
                                                   stat[:, 3, c:c + 1], ALU.subtract, ALU.mult)
                last.then_inc(p_step, 1)
                pool.wait_ge(p_step, q + 1)
                nc.gpsimd.tensor_scalar(h_sb[:, p0:c1, :], tmp_n[:, p0:c1, :], 0.0, None,
                                        ALU.max).then_inc(h_pool, 1)
            pool.wait_ge(h_out, 32 * len(CHUNKS))
            gather(0, 0, HTILES)
            gather(0, 1, HTILES - PEG[1])
            with pool.Fori(1, UNITS) as u:
                gather(u, 0, HTILES - PEG[0])
                gather(u, 1, HTILES - PEG[1])
            gather(UNITS, 0, TILES - UNITS * UNIT * BLOCK)
            with pool.If(flag_on(pool) > 0):
                pool.wait_ge(msg_done, BLOCKS)

                def gather_tile(t):
                    wait_count(pool, m_msg, t)
                    pool.wait_ge(m_idx, 16 * t + 16)
                    pool.nop(nofuse=True)
                    pool.indirect_dma_start(
                        g_sb[0][:, 0, :], None, h_dram[:, :],
                        bass.IndirectOffsetOnAxis(ap=idx_one[:, :], axis=0)).then_inc(m_gather, 16)

                gather_tile(0)
                with pool.Fori(1, TILES) as t:
                    gather_tile(t)

        @block.scalar
        def _(act):
            a = nc.scalar
            act.wait_ge(eps_set, 1)
            a.activation(eps[:, 1:2], eps[:, 0:1], ACT.Sqrt)
            act.wait_ge(var_done, 1)
            a.activation(stat[:, 5, :], stat[:, 4, :], ACT.Sqrt, bias=eps[0:NP, 0:1],
                         scale=1.0 / D).then_inc(std_done, 1)
            act.wait_ge(shift_done, 1)
            for (c0, c1), (dve_cols, act_cols, _) in zip(CHUNKS, SHARES):
                for c in range(c0 + dve_cols, c0 + dve_cols + act_cols):
                    last = a.activation(h_sb[:, c, :], x_sb[:, c, :], ACT.Relu, bias=stat[:, 0, c:c + 1],
                                        scale=stat[:, 3, c:c + 1])
                last.then_inc(h_act, 1)
            act.wait_ge(w_in, 96)
            a.copy(w1_hi[:, :], w1_sb[:, :]).then_inc(whi_done, 1)
            act.wait_ge(wr_done, 1)
            a.copy(w1_mid[:, :], w1_r[:, :]).then_inc(wmid_done, 1)

            def attr_hi(u, k):
                act.wait_ge(nat_in[k], 16 * u + 16)
                wait_count(act, t_done, HALF * (2 * u + k - 1))
                a.copy(stack[k][:, :, 0:3 * ED].rearrange("p t (n f) -> p t n f", n=3),
                       nat[k][:, :, :].unsqueeze(2).broadcast_to([P, HTILES, 3, ED])).then_inc(ahi_done, 1)

            def attr_mid(u, k):
                act.wait_ge(ar_done, 2 * u + k + 1)
                a.copy(stack[k][:, :, 3 * ED:6 * ED].rearrange("p t (n f) -> p t n f", n=3),
                       nat_r[:, :, :].unsqueeze(2).broadcast_to([P, HTILES, 3, ED])).then_inc(amid_done, 1)

            def copy_stack(u, s):
                b = UNIT * u + s
                act.wait_ge(t_done, b + 1)
                wait_count(act, l1_done, b - 1)
                a.copy(stackT[s % 2][:, :], ps_t[0:KS, 0:BLOCK * TILE]).then_inc(copy_done, 1)

            def relu(u, s):
                b = UNIT * u + s
                act.wait_ge(l1_done, b + 1)
                wait_count(act, l2_done, b - 1)
                a.activation(r_sb[s % 2][0:D, :], ps_l1[s % 2][0:D, :], ACT.Relu).then_inc(relu_done, 1)

            def node_evacuate(i):
                act.wait_ge(node_ps, i + 1)
                n = min(4, NC - 4 * i)
                a.copy(hT[0:D, 4 * i:4 * i + n, :],
                       ps_g[i % 2][0:D, 0:n * NP].rearrange("p (c n) -> p c n", c=n)).then_inc(node_sb, 1)

            def turn(u, s, last=False):
                k, q = s // HALF, s % HALF
                if not last or s + 1 < REST:
                    copy_stack(*((u, s + 1) if s + 1 < UNIT else (u + 1, 0)))
                early = known(u) and u == 0 and s < HALF
                if early:
                    node_evacuate(2 * s)
                relu(u, s)
                if q == 0 and not last:
                    attr_hi(*((u + 1, 0) if k else (u, 1)))
                if q == 1 and not last:
                    attr_mid(*((u + 1, 0) if k else (u, 1)))
                if early and 2 * s + 1 < NODE_TASKS:
                    node_evacuate(2 * s + 1)

            attr_hi(0, 0)
            attr_mid(0, 0)
            copy_stack(0, 0)
            for s in range(UNIT):
                if s == 1:
                    act.wait_ge(h_dve, len(CHUNKS))
                    act.wait_ge(h_pool, len(CHUNKS))
                    a.copy(h_part[:, :, 0], h_sb[:, :, :]).then_inc(hhi_done, 1)
                if s == 3:
                    act.wait_ge(hr_done, 1)
                    a.copy(h_part[:, :, 1], tmp_n[:, :, :]).then_inc(hmid_done, 1)
                turn(0, s)
            with act.Fori(1, UNITS) as u:
                for s in range(UNIT):
                    turn(u, s)
            for s in range(REST):
                turn(UNITS, s, last=True)
            with act.If(flag_on(act) > 0):
                def tile_step(t):
                    act.wait_ge(m_t, t + 1)
                    wait_count(act, m_l1, t)
                    a.copy(natT_one[:, :], one_t).then_inc(m_copy, 1)
                    act.wait_ge(m_l1, t + 1)
                    wait_count(act, m_l2, t)
                    a.activation(r_sb[0][0:D, 0:TILE], one_l1, ACT.Relu,
                                 bias=b1_sb[:, 0:1]).then_inc(m_relu, 1)

                tile_step(0)
                with act.Fori(1, TILES) as t:
                    tile_step(t)

        @block.tensor
        def _(pe):
            mm = nc.tensor.matmul
            pe.wait_ge(ones_set, 1)
            pe.wait_ge(dstf_ready, 1)
            mm(ps_l2[0][:, 0:BPAD], ones[0:1, :], dstf[0:1, 0:TPAD:BLOCK], start=True, stop=True).then_inc(base_ps, 1)
            pe.wait_ge(const_rows, 4)
            pe.wait_ge(idents, 2)
            pe.wait_ge(w_in, 96)
            pe.wait_ge(base_read, 1)
            pe.wait_ge(w1_ready, 1)

            def node_task(i):
                wait_count(pe, node_sb, i - 1)
                for c in range(min(4, NC - 4 * i)):
                    last = nc.tensor.transpose(ps_g[i % 2][0:D, c * NP:(c + 1) * NP], h_sb[:, 4 * i + c, :],
                                               ident[0:NP, 0:NP])
                last.then_inc(node_ps, 1)

            def own(q):
                for c in range(5):
                    mm(ps_out[q][0:NP, c * D:(c + 1) * D], hT[:, 5 * q + c, :], ws_sb[:, :],
                       start=(c == 0), stop=False)

            def transpose(u, s):
                b = UNIT * u + s
                if s % HALF == 0:
                    pe.wait_ge(stack_done, 2 * u + s // HALF + 1)
                wait_count(pe, copy_done, b)
                for j in range(BLOCK):
                    last = nc.tensor.transpose(ps_t[0:KS, j * TILE:(j + 1) * TILE],
                                               stack[s // HALF][:, (s % HALF) * BLOCK + j, :], ident_b[:, :])
                last.then_inc(t_done, 1)

            def layer1(u, s):
                b = UNIT * u + s
                pe.wait_ge(copy_done, b + 1)
                wait_count(pe, relu_done, b - 1)
                mm(ps_l1[s % 2][0:D, :], w1_s[:, :], stackT[s % 2][:, :], start=True, stop=True).then_inc(l1_done, 1)

            def layer2(u, s):
                b = UNIT * u + s
                pe.wait_ge(relu_done, b + 1)
                wait_count(pe, msg_done, b - 1)
                for j in range(BLOCK):
                    last = mm(ps_l2[s % 2][:, j * D:(j + 1) * D], r_sb[s % 2][:, j * TILE:(j + 1) * TILE],
                              w2_sb[:, :], start=True, stop=True)
                last.then_inc(l2_done, 1)

            def scatter(u, s):
                b = UNIT * u + s
                pe.wait_ge(msg_done, b + 1)
                pe.wait_ge(hot_done, b + 1)
                wait_count(pe, agg_done, b)
                for j in range(BLOCK):
                    last = mm(ps_ag[0:D, 0:WIN], msg[s % 2][:, j, :], hot[s % 2][:, j, :],
                              start=(j == 0), stop=(j == BLOCK - 1))
                last.then_inc(scat_done, 1)

            def gather(u, s):
                k, q = s // HALF, s % HALF
                if q == 0:
                    pe.wait_ge(pick_done, 2 * u + k + 1)
                for j, c in peg_slices(k)[q]:
                    ps = ps_g[peg_bank(k, j)]
                    if c == 0:
                        wait_count(pe, evac_done, peg_before(u, k) + j - peg_reuse(k, j) + 1)
                    at = PMAX - PEG[k] + j
                    last = mm(ps[:, 0:NPARTS * D], pick[k][:, c, at * TILE:(at + 1) * TILE],
                              h_part[:, c].rearrange("p n f -> p (n f)"), start=(c == 0), stop=(c == NC - 1))
                    if c == NC - 1:
                        last.then_inc(peg_done, 1)

            def turn(u, s, last=False):
                if not last or s + 1 < REST:
                    transpose(*((u, s + 1) if s + 1 < UNIT else (u + 1, 0)))
                early = known(u) and u == 0 and s < HALF
                if early:
                    node_task(2 * s)
                layer1(u, s)
                if not (known(u) and UNIT * u + s < 1):
                    layer2(*((u, s - 1) if s >= 1 else (u - 1, s + UNIT - 1)))
                if not (known(u) and UNIT * u + s < 2):
                    scatter(*((u, s - 2) if s >= 2 else (u - 1, s + UNIT - 2)))
                if early:
                    if 2 * s + 1 < NODE_TASKS:
                        node_task(2 * s + 1)
                elif not last:
                    gather(u, s)

            transpose(0, 0)
            for s in range(UNIT):
                if s == 0:
                    for part in (h_dve, h_act, h_pool):
                        pe.wait_ge(part, len(CHUNKS))
                if s == HALF:
                    pe.wait_ge(h_parts, 1)
                    pe.wait_ge(node_sb, NODE_TASKS)
                    pe.wait_ge(outside_ready, 1)
                    for k in range(2):
                        last = mm(ps_count, outside[:, k:k + 1], ones[:, 0:1], start=(k == 0), stop=(k == 1))
                    last.then_inc(count_ps, 1)
                if s == HALF + 1:
                    pe.wait_ge(flag_ready, 1)
                turn(0, s)
            with pe.Fori(1, UNITS) as u:
                for s in range(UNIT):
                    turn(u, s)
            pe.wait_ge(own_rows, 1)
            for s in range(REST):
                turn(UNITS, s, last=True)
                if s == 0:
                    pe.wait_ge(evac_done, peg_before(UNITS, 0))
                    own(0)
                    own(1)
            layer2(UNITS, REST - 1)
            pe.wait_ge(relu_done, BLOCKS)
            own(2)
            scatter(UNITS, REST - 2)
            scatter(UNITS, REST - 1)
            own(3)
            pe.wait_ge(msg_done, BLOCKS - 1)
            own(4)
            with pe.If(flag_on(pe) > 0):
                pe.wait_ge(agg_done, BLOCKS)

                def tile_step(t):
                    pe.wait_ge(m_nat, 16 * t + 16)
                    wait_count(pe, m_msg, t)
                    nc.tensor.transpose(one_t, nat_one[:, :], ident[:, :]).then_inc(m_t, 1)
                    pe.wait_ge(m_copy, t + 1)
                    mm(one_l1, w1_sb[0:ED, :], natT_one[:, :], start=True, stop=True).then_inc(m_l1, 1)
                    pe.wait_ge(m_relu, t + 1)
                    mm(one_l2, r_sb[0][:, 0:TILE], w2_sb[:, :], start=True, stop=True).then_inc(m_l2, 1)
                    pe.wait_ge(m_msg, t + 1)
                    for w in range(SWEEPS):
                        pe.wait_ge(m_hot, SWEEPS * t + w + 1)
                        wait_count(pe, m_agg, SWEEPS * t + w)
                        mm(ps_ag[0:D, :], msg[0][:, 0, :], hot_sweep[:, :], start=True, stop=True).then_inc(m_scat, 1)

                tile_step(0)
                with pe.Fori(1, TILES) as t:
                    tile_step(t)
                pe.wait_ge(m_agg, SWEEPS * TILES)
            pe.wait_ge(agg_done, BLOCKS)
            for q in range(NQ):
                for c in range(5):
                    last = mm(ps_out[q][0:NP, c * D:(c + 1) * D], aggT[:, 5 * q + c:N:NC], wn_sb[:, :],
                              start=False, stop=(c == 4))
                last.then_inc(out_ps, 1)

        @block.vector
        def _(dve):
            v = nc.vector
            steps = [0]

            def step(ins):
                steps[0] += 1
                ins.then_inc(v_step, 1)
                dve.wait_ge(v_step, steps[0])

            v.memset(eps[:, 0:1], 1e-5).then_inc(eps_set, 1)
            for k in range(2):
                v.memset(r_sb[k][D:D + 1, :], 1.0).then_inc(const_rows, 1)
                v.memset(stack[k][:, :, KA:KS], 1.0).then_inc(const_rows, 1)
            for q, (c0, c1) in enumerate(CHUNKS):
                dve.wait_ge(x_in[q], 32)
                for c in range(c0, c1):
                    last = v.bn_stats(stats[:, c, :], x_sb[:, c, :])
            step(last)
            mean_e, mean_o = stats[:, :, 1], stats[:, :, 4]
            v.tensor_tensor(stat[:, 0, :], mean_e, mean_o, ALU.add)
            step(v.tensor_tensor(stat[:, 1, :], mean_e, mean_o, ALU.subtract))
            v.tensor_tensor(stat[:, 2, :], stats[:, :, 2], stats[:, :, 5], ALU.add)
            step(v.tensor_tensor(stat[:, 3, :], stat[:, 1, :], stat[:, 1, :], ALU.mult))
            v.scalar_tensor_tensor(stat[:, 4, :], stat[:, 3, :], D / 4.0, stat[:, 2, :], ALU.mult,
                                   ALU.add).then_inc(var_done, 1)
            v.tensor_scalar(stat[:, 1, :], stat[:, 0, :], 0.5, None, ALU.mult).then_inc(mean_done, 1)
            dve.wait_ge(mean_done, 1)
            dve.wait_ge(std_done, 1)
            v.reciprocal(stat[:, 3, :], stat[:, 5, :]).then_inc(scale_done, 1)
            dve.wait_ge(scale_done, 1)
            v.scalar_tensor_tensor(stat[:, 0, :], stat[:, 1, :], -1.0, stat[:, 3, :], ALU.mult,
                                   ALU.mult).then_inc(shift_done, 1)
            for (c0, _), (dve_cols, _, _) in zip(CHUNKS, SHARES):
                c1 = c0 + dve_cols
                for c in range(c0, c1):
                    last = v.tensor_scalar(tmp_n[:, c, :], x_sb[:, c, :], stat[:, 1, c:c + 1], stat[:, 3, c:c + 1],
                                           ALU.subtract, ALU.mult)
                step(last)
                v.tensor_scalar(h_sb[:, c0:c1, :], tmp_n[:, c0:c1, :], 0.0, None, ALU.max).then_inc(h_dve, 1)
            dve.wait_ge(iota_set, 3)
            v.tensor_scalar(ident[:, :], diff[:, :], 0.0, None, ALU.is_equal).then_inc(idents, 1)
            v.tensor_scalar(ident_b[:, :], diff[:, :], 0.0, None, ALU.is_equal).then_inc(idents, 1)
            v.tensor_copy(first[:, :], first_i[:, :]).then_inc(srcx_done, 1)
            v.tensor_copy(iota_f[:, :], iota_i[:, :]).then_inc(pick_done, 1)

            dve.wait_ge(dst_in, 16)
            v.tensor_copy(dstf[:, :], dst_sb[:, :]).then_inc(dstf_ready, 1)
            dve.wait_ge(base_ps, 1)
            v.tensor_scalar(base_b[:, :], ps_l2[0][:, 0:BPAD], 0.0, None, ALU.max).then_inc(base_read, 1)
            dve.wait_ge(base_read, 1)
            step(v.tensor_copy(base_i[:, :], base_b[0:1, :]))
            step(v.tensor_tensor(local[:, :].rearrange("p (g j) -> p g j", j=BLOCK),
                                 dstf[:, :].rearrange("p (g j) -> p g j", j=BLOCK),
                                 base_b[:, :].unsqueeze(2).broadcast_to([P, BPAD, BLOCK]), ALU.subtract))
            dve.wait_ge(whi_done, 1)
            v.tensor_tensor(w1_r[:, :], w1_sb[:, :], w1_hi[:, :], ALU.subtract).then_inc(wr_done, 1)

            def attr_r(u, k):
                h = 2 * u + k
                dve.wait_ge(ahi_done, h + 1)
                wait_count(dve, amid_done, h)
                v.tensor_tensor(nat_r[:, :, :], nat[k][:, :, :], stack[k][:, :, 0:ED],
                                ALU.subtract).then_inc(ar_done, 1)

            def attr_lo(u, k):
                h = 2 * u + k
                dve.wait_ge(amid_done, h + 1)
                v.tensor_tensor(stack[k][:, :, 6 * ED:7 * ED], nat_r[:, :, :], stack[k][:, :, 3 * ED:4 * ED],
                                ALU.subtract).then_inc(stack_done, 1)

            def src_offsets(u, k):
                h = 2 * u + k
                dve.wait_ge(srcb_in[k], 16 * (u + k))
                wait_count(dve, pick_done, h - 1)
                v.tensor_scalar(srcx[k][:, :], srcb[k][:, :], first[0:NP, 0:1], None,
                                ALU.subtract).then_inc(srcx_done, 1)
                dve.wait_ge(srcx_done, h + 1)

            def picks(u, k, q, part):
                h = 2 * u + k
                if q == 0 and part == 0:
                    wait_count(dve, peg_done, peg_before(u - 1, k) + PEG[k])
                cols = slice((PMAX - PEG[k]) * TILE, PICKS)
                c0, c1 = NC * q // HALF, NC * (q + 1) // HALF
                mid = c1 - PICKS_LATE
                for c in range(mid, c1) if part else range(c0, mid):
                    last = v.tensor_scalar(pick[k][:, c, cols], srcx[k][:, cols], float(c), None, ALU.is_equal)
                if q == HALF - 1 and part:
                    last.then_inc(pick_done, 1)

            def message(u, s):
                b, k, q = UNIT * u + s, s // HALF, s % HALF
                dve.wait_ge(l2_done, b + 1)
                dve.wait_ge(gathered[s], landed(u, s))
                if q == HALF - 1:
                    wait_count(dve, evac_done, peg_before(u, k) + PEG[k])
                wait_count(dve, scat_done, b - 1)
                v.tensor_tensor(msg[s % 2][:, :, :],
                                ps_l2[s % 2][:, 0:BLOCK * D].rearrange("p (j f) -> p j f", j=BLOCK),
                                g_sb[k][:, q * BLOCK:(q + 1) * BLOCK, :], ALU.mult).then_inc(msg_done, 1)

            def evacuate(u, k, j):
                dve.wait_ge(peg_done, peg_before(u, k) + j + 1)
                wait_count(dve, msg_done, HALF * (2 * u + k))
                v.tensor_reduce(g_sb[k][:, HTILES - PEG[k] + j, :],
                                ps_g[peg_bank(k, j)][:, 0:NPARTS * D].rearrange("p (n f) -> p f n", n=NPARTS),
                                AX.X, ALU.add).then_inc(evac_done, 1)

            def one_hot(u, s):
                b = UNIT * u + s
                wait_count(dve, scat_done, b - 1)
                v.tensor_tensor(hot[s % 2][:, :, :],
                                local[:, bass.ds(b * BLOCK, BLOCK)].unsqueeze(2).broadcast_to([P, BLOCK, WIN]),
                                iota_f[:, 0:WIN].unsqueeze(1).broadcast_to([P, BLOCK, WIN]),
                                ALU.is_equal).then_inc(hot_done, 1)

            def window(u, s):
                return dve.value_load(base_i[0:1, bass.ds(UNIT * u + s, 1)], min_val=0, max_val=N - 1)

            def aggregate(u, s, at):
                b = UNIT * u + s
                dve.wait_ge(scat_done, b + 1)
                wait_count(dve, agg_done, b)
                win = aggT[:, bass.ds(at, WIN)]
                v.tensor_tensor(win, win, ps_ag[0:D, 0:WIN], ALU.add).then_inc(agg_done, 1)

            def turn(u, s, last=False):
                k, q = s // HALF, s % HALF
                nu, nk = (u, 1) if s < HALF else (u + 1, 0)
                pu, ps = (u, s - 1) if s else (u - 1, UNIT - 1)
                qu, qs = (u, s - 2) if s >= 2 else (u - 1, s + UNIT - 2)
                adds = not (known(u) and UNIT * u + s < 2)
                before = not (known(u) and UNIT * u + s == 0)
                more = not last and not (known(u) and u == UNITS)
                eu, ek, eq = (u, k, q - 1) if q else (u, 0, HALF - 1) if k else (u - 1, 1, HALF - 1)
                if q == 0:
                    for j in peg_ends(ek, eq) if not known(eu) or 0 < 2 * eu + ek else []:
                        evacuate(eu, ek, j)
                if before:
                    message(pu, ps)
                if q:
                    for j in peg_ends(ek, eq) if not (last or known(eu) and 2 * eu + ek == 0) else []:
                        evacuate(eu, ek, j)
                if q == 0 and more:
                    src_offsets(nu, nk)
                if q == 1 and more:
                    attr_r(nu, nk)
                if q == 2 and more:
                    attr_lo(nu, nk)
                if before:
                    one_hot(pu, ps)
                if more:
                    picks(nu, nk, q, 0)
                if adds:
                    at = window(qu, qs)
                if more:
                    picks(nu, nk, q, 1)
                if adds:
                    aggregate(qu, qs, at)

            attr_r(0, 0)
            dve.wait_ge(wmid_done, 1)
            step(v.tensor_tensor(w1_r[:, :], w1_r[:, :], w1_mid[:, :], ALU.subtract))
            step(v.tensor_scalar(w1_r[:, :], w1_r[:, :], w1_pick[:, 2:3], None, ALU.mult))
            step(v.scalar_tensor_tensor(w1_r[:, :], w1_mid[:, :], w1_pick[:, 1:2], w1_r[:, :], ALU.mult, ALU.add))
            v.scalar_tensor_tensor(w1_s[:, :], w1_hi[:, :], w1_pick[:, 0:1], w1_r[:, :], ALU.mult,
                                   ALU.add).then_inc(w1_ready, 1)
            attr_lo(0, 0)
            dve.wait_ge(agg_zero, 1)
            for s in range(UNIT):
                if s == 1:
                    step(v.tensor_scalar(off[:, :], local[:, :], float(WIN), 0.0, ALU.is_ge, ALU.add,
                                         accum_out=outside[:, 0:1]))
                    v.tensor_scalar(off[:, :], local[:, :], 0.0, 0.0, ALU.is_lt, ALU.add,
                                    accum_out=outside[:, 1:2]).then_inc(outside_ready, 1)
                if s == 5:
                    dve.wait_ge(count_ps, 1)
                    v.tensor_scalar(misfits[:, :], ps_count, float(-PADS), None,
                                    ALU.add).then_inc(flag_ready, 1)
                if s == 6:
                    v.memset(hT[D:D + 2, :, :], 1.0).then_inc(own_rows, 1)
                if s == 2:
                    dve.wait_ge(hhi_done, 1)
                    dve.wait_ge(h_act, len(CHUNKS))
                    dve.wait_ge(h_pool, len(CHUNKS))
                    v.tensor_tensor(tmp_n[:, :, :], h_sb[:, :, :], h_part[:, :, 0], ALU.subtract).then_inc(hr_done, 1)
                if s == 4:
                    dve.wait_ge(hmid_done, 1)
                    v.tensor_tensor(h_part[:, :, 2], tmp_n[:, :, :], h_part[:, :, 1], ALU.subtract).then_inc(h_parts, 1)
                turn(0, s)
            with dve.Fori(1, UNITS) as u:
                for s in range(UNIT):
                    turn(u, s)
            for s in range(REST):
                turn(UNITS, s, last=True)
            message(UNITS, REST - 1)
            one_hot(UNITS, REST - 1)
            for b in range(BLOCKS - 2, BLOCKS):
                aggregate(b // UNIT, b % UNIT, window(b // UNIT, b % UNIT))
            with dve.If(flag_on(dve) > 0):
                dve.wait_ge(agg_done, BLOCKS)
                masks = [0]

                def mask(ins):
                    masks[0] += 1
                    ins.then_inc(m_mask, 1)
                    dve.wait_ge(m_mask, masks[0])

                mask(v.tensor_scalar(off[:, :], local[:, :], 0.0, None, ALU.is_ge))
                mask(v.scalar_tensor_tensor(off[:, :], local[:, :], float(WIN), off[:, :], ALU.is_lt, ALU.mult))
                mask(v.tensor_scalar(local[:, :], dstf[:, :], 1.0, None, ALU.add))
                mask(v.tensor_tensor(off[:, :], off[:, :], local[:, :], ALU.mult))
                mask(v.tensor_tensor(dstf[:, :], dstf[:, :], off[:, :], ALU.subtract))

                def tile_step(t):
                    v.tensor_copy(dst_one[:, :], dstf[:, bass.ds(t, 1)]).then_inc(m_dst, 1)
                    dve.wait_ge(m_l2, t + 1)
                    dve.wait_ge(m_gather, 16 * t + 16)
                    wait_count(dve, m_scat, SWEEPS * t)
                    v.tensor_tensor(msg[0][:, 0, :], one_l2, g_sb[0][:, 0, :],
                                    ALU.mult).then_inc(m_msg, 1)
                    dve.wait_ge(m_dst, t + 1)
                    for w in range(SWEEPS):
                        wait_count(dve, m_scat, SWEEPS * t + w)
                        v.tensor_scalar(hot_sweep[:, :], iota_f[:, :], dst_one[:, 0:1], float(-w * SWEEP),
                                        ALU.subtract, ALU.is_equal).then_inc(m_hot, 1)
                        dve.wait_ge(m_scat, SWEEPS * t + w + 1)
                        wait_count(dve, m_agg, SWEEPS * t + w)
                        win = aggT[:, w * SWEEP:(w + 1) * SWEEP]
                        v.tensor_tensor(win, win, ps_ag[0:D, :], ALU.add).then_inc(m_agg, 1)

                tile_step(0)
                with dve.Fori(1, TILES) as t:
                    tile_step(t)
            for q in range(NQ):
                dve.wait_ge(out_ps, q + 1)
                cs = slice(5 * q, 5 * q + 5)
                v.scalar_tensor_tensor(h_sb[:, cs, :], ps_out[q][0:NP, 0:5 * D].rearrange("p (c f) -> p c f", c=5),
                                       0.0, x_sb[:, cs, :], ALU.max, ALU.add).then_inc(out_ready, 1)


def kernel(x, src, dst, edge_attr_17, L0_gnn_W1, L0_gnn_b1, L0_gnn_W2, L0_gnn_b2, L0_gnn_Ws, L0_gnn_bs,
           L0_gnn_Wn, L0_gnn_bn):
    import numpy as np
    import concourse.bacc as bacc
    from concourse.bass_utils import run_bass_kernel_spmd

    def padded(a, fill):
        a = np.asarray(a)
        return np.concatenate([a, np.full((PADS, *a.shape[1:]), fill, a.dtype)])

    def by_half(a, fill):
        a = padded(a, fill)
        return np.ascontiguousarray(a.reshape(HALVES, HTILES, TILE, *a.shape[1:]).swapaxes(1, 2))

    src_h, dst_h = by_half(src, 0), by_half(dst, -1)
    b1, b2, bs, bn = (np.asarray(b)[None, :] for b in (L0_gnn_b1, L0_gnn_b2, L0_gnn_bs, L0_gnn_bn))
    w1_t = np.asarray(L0_gnn_W1).T
    parts = np.concatenate([np.repeat(W_PART, ED), np.arange(NPARTS)])
    arrays = {
        "x_in": np.ascontiguousarray(x),
        "src_half": src_h,
        "src_rows": padded(src, 0).reshape(TPAD, TILE),
        "dst_tiles": np.ascontiguousarray(dst_h.swapaxes(0, 1).reshape(TILE, TPAD)),
        "attr_half": by_half(edge_attr_17, 0),
        "attr_rows": padded(edge_attr_17, 0),
        "w1_rows": np.concatenate([w1_t] * len(W_PART) + [b1] * NPARTS),
        "w1_part": (parts[:, None] == np.arange(NPARTS)[None, :]).astype(np.float32),
        "b1_col": np.ascontiguousarray(b1.T),
        "w2_t": np.concatenate([np.asarray(L0_gnn_W2).T, b2]),
        "ws_t": np.concatenate([np.asarray(L0_gnn_Ws).T, bs, bn]),
        "wn_t": np.ascontiguousarray(np.asarray(L0_gnn_Wn).T),
    }
    nc = bacc.Bacc("TRN2", target_bir_lowering=False, num_devices=1)
    args = [nc.dram_tensor(n, a.shape, mybir.dt.from_np(a.dtype), kind="ExternalInput").ap()
            for n, a in arrays.items()]
    out = nc.dram_tensor("out_rows", [N, D], mybir.dt.float32, kind="ExternalOutput").ap()
    gnn_layer(nc, *args, out)
    r = run_bass_kernel_spmd(nc, [arrays], core_ids=[0])
    return r.results[0]["out_rows"]
```
